# Optimizing a Trainium2 kernel written in Bass

```python
import numpy as np
import jax
import jax.numpy as jnp

def _softmax(x, axis=-1):
    return jax.nn.softmax(x, axis=axis)

def _gelu(x):
    return jax.nn.gelu(x, approximate=True)

def _silu(x):
    return jax.nn.silu(x)

def _sigmoid(x):
    return jax.nn.sigmoid(x)

def _layernorm(x, axis=-1, eps=1e-05):
    m = jnp.mean(x, axis=axis, keepdims=True)
    v = jnp.var(x, axis=axis, keepdims=True)
    return (x - m) / jnp.sqrt(v + eps)

def _scatter_add(tgt, idx, src, axis=0):
    return tgt.at[idx].add(src)

def _segment_sum(src, seg, n):
    return jax.ops.segment_sum(src, seg, n)
kernel_name = 'mk_seq_preln_d1_jaxref_r8_59ac3a'

def setup_inputs(seed: int=0):
    np.random.seed(seed)
    _w = jnp.asarray

    def _L0_attn_setup():
        import jax, jax.numpy as jnp
        import numpy as np
        DIM = 128
        HEADS = 8
        DIM_QK = 64
        MAX_POS = 10
        SCALE = DIM_QK ** (-0.5)
        key = jax.random.key(seed)
        ks = jax.random.split(key, 6)
        b, n = (4, 256)
        x = jax.random.normal(ks[0], (b, n, DIM), dtype=jnp.float32)
        mask = jnp.ones((b, n), dtype=bool)
        s = DIM ** (-0.5)
        W_qk = jax.random.normal(ks[1], (DIM, DIM_QK * HEADS * 2), dtype=jnp.float32) * s
        W_v = jax.random.normal(ks[2], (DIM, DIM), dtype=jnp.float32) * s
        W_out = jax.random.normal(ks[3], (DIM, DIM), dtype=jnp.float32) * s
        b_out = jnp.zeros((DIM,), dtype=jnp.float32)
        conv = jax.random.normal(ks[4], (HEADS, 2 * MAX_POS + 1), dtype=jnp.float32) * 0.02
        return {'x': x, 'mask': mask, 'W_qk': W_qk, 'W_v': W_v, 'W_out': W_out, 'b_out': b_out, 'conv': conv}
    _L0_attn_in = _L0_attn_setup()

    def _L0_ffn_setup():
        import jax, jax.numpy as jnp
        import numpy as np
        NUM_NOD = 6
        MAX_PREV = 5
        NUM_EDGE = 20
        D = 128
        H = 8
        LN_EPS = 1e-06

        def _layernorm(x, g, b):
            mu = jnp.mean(x, axis=-1, keepdims=True)
            var = jnp.mean(jnp.square(x - mu), axis=-1, keepdims=True)
            return (x - mu) * jax.lax.rsqrt(var + LN_EPS) * g + b

        def _mha(q, k, v, wq, wk, wv, wo):
            B, S, d = q.shape
            dh = d // H
            qh = (q @ wq).reshape(B, S, H, dh)
            kh = (k @ wk).reshape(B, S, H, dh)
            vh = (v @ wv).reshape(B, S, H, dh)
            scores = jnp.einsum('bqhd,bkhd->bhqk', qh, kh) / jnp.sqrt(jnp.asarray(dh, q.dtype))
            attn = jax.nn.softmax(scores, axis=-1)
            ctx = jnp.einsum('bhqk,bkhd->bqhd', attn, vh).reshape(B, S, d)
            return ctx @ wo
        key = jax.random.key(seed)
        ks = jax.random.split(key, 12)
        B, S = (8, 128)
        scale = 1.0 / np.sqrt(D)
        return {'inputs': jax.random.normal(ks[0], (B, S, D), jnp.float32), 'ew': jax.random.uniform(ks[1], (NUM_NOD, 3), jnp.float32), 'act_w': jax.random.uniform(ks[2], (NUM_NOD,), jnp.float32), 'We': jax.random.normal(ks[3], (NUM_EDGE, D, D), jnp.float32) * scale, 'be': jnp.zeros((NUM_EDGE, D), jnp.float32), 'Wq': jax.random.normal(ks[4], (NUM_NOD, D, D), jnp.float32) * scale, 'Wk': jax.random.normal(ks[5], (NUM_NOD, D, D), jnp.float32) * scale, 'Wv': jax.random.normal(ks[6], (NUM_NOD, D, D), jnp.float32) * scale, 'Wo': jax.random.normal(ks[7], (NUM_NOD, D, D), jnp.float32) * scale, 'ln_g': jnp.ones((D,), jnp.float32), 'ln_b': jnp.zeros((D,), jnp.float32)}
    _L0_ffn_in = _L0_ffn_setup()
    _d = {'L0_attn_x': _L0_attn_in['x'], 'L0_attn_mask': _L0_attn_in['mask'], 'L0_attn_W_qk': _L0_attn_in['W_qk'], 'L0_attn_W_v': _L0_attn_in['W_v'], 'L0_attn_W_out': _L0_attn_in['W_out'], 'L0_attn_b_out': _L0_attn_in['b_out'], 'L0_attn_conv': _L0_attn_in['conv'], 'L0_ffn_ew': _L0_ffn_in['ew'], 'L0_ffn_act_w': _L0_ffn_in['act_w'], 'L0_ffn_We': _L0_ffn_in['We'], 'L0_ffn_be': _L0_ffn_in['be'], 'L0_ffn_Wq': _L0_ffn_in['Wq'], 'L0_ffn_Wk': _L0_ffn_in['Wk'], 'L0_ffn_Wv': _L0_ffn_in['Wv'], 'L0_ffn_Wo': _L0_ffn_in['Wo'], 'L0_ffn_ln_g': _L0_ffn_in['ln_g'], 'L0_ffn_ln_b': _L0_ffn_in['ln_b']}
    _x0 = _d['L0_attn_x']
    _d['L0_attn_x'] = jax.random.normal(jax.random.fold_in(jax.random.key(seed), 1), (4, 1024, 128), dtype=_x0.dtype)
    del _x0
    return _d

def reference(L0_attn_x, L0_attn_mask, L0_attn_W_qk, L0_attn_W_v, L0_attn_W_out, L0_attn_b_out, L0_attn_conv, L0_ffn_ew, L0_ffn_act_w, L0_ffn_We, L0_ffn_be, L0_ffn_Wq, L0_ffn_Wk, L0_ffn_Wv, L0_ffn_Wo, L0_ffn_ln_g, L0_ffn_ln_b):

    def _L0_attn_ref(x, mask, W_qk, W_v, W_out, b_out, conv):
        import jax, jax.numpy as jnp
        import numpy as np
        DIM = 128
        HEADS = 8
        DIM_QK = 64
        MAX_POS = 10
        SCALE = DIM_QK ** (-0.5)
        b, n, _ = x.shape
        h, dqk = (HEADS, DIM_QK)
        dv = DIM // h
        qk = x @ W_qk
        q, k = jnp.split(qk, 2, axis=-1)
        v = x @ W_v
        q = q.reshape(b, n, h, dqk).transpose(0, 2, 1, 3)
        k = k.reshape(b, n, h, dqk).transpose(0, 2, 1, 3)
        v = v.reshape(b, n, h, dv).transpose(0, 2, 1, 3)
        dots = jnp.einsum('bhid,bhjd->bhij', q, k) * SCALE
        seq = jnp.arange(n)
        dist = jnp.clip(seq[None, :] - seq[:, None], -MAX_POS, MAX_POS) + MAX_POS
        bias = conv[:, dist]
        attn = jax.nn.softmax(dots + bias[None], axis=-1)
        out = jnp.einsum('bhij,bhjd->bhid', attn, v)
        out = out.transpose(0, 2, 1, 3).reshape(b, n, h * dv)
        return out @ W_out + b_out

    def _L0_ffn_ref(inputs, ew, act_w, We, be, Wq, Wk, Wv, Wo, ln_g, ln_b):
        import jax, jax.numpy as jnp
        import numpy as np
        NUM_NOD = 6
        MAX_PREV = 5
        NUM_EDGE = 20
        D = 128
        H = 8
        LN_EPS = 1e-06

        def _layernorm(x, g, b):
            mu = jnp.mean(x, axis=-1, keepdims=True)
            var = jnp.mean(jnp.square(x - mu), axis=-1, keepdims=True)
            return (x - mu) * jax.lax.rsqrt(var + LN_EPS) * g + b

        def _mha(q, k, v, wq, wk, wv, wo):
            B, S, d = q.shape
            dh = d // H
            qh = (q @ wq).reshape(B, S, H, dh)
            kh = (k @ wk).reshape(B, S, H, dh)
            vh = (v @ wv).reshape(B, S, H, dh)
            scores = jnp.einsum('bqhd,bkhd->bhqk', qh, kh) / jnp.sqrt(jnp.asarray(dh, q.dtype))
            attn = jax.nn.softmax(scores, axis=-1)
            ctx = jnp.einsum('bhqk,bkhd->bqhd', attn, vh).reshape(B, S, d)
            return ctx @ wo
        nodes = {-1: inputs}
        lind = 0
        for c in range(NUM_NOD):
            nsrc = min(c + 1, MAX_PREV)
            snode = c - nsrc
            eq, ek, ev = (lind + nsrc - 1, lind, lind + nsrc // 2)
            in_q, in_k, in_v = (c - 1, snode, snode + nsrc // 2)
            q = ew[c, 0] * (nodes[in_q] @ We[eq] + be[eq])
            k = ew[c, 1] * (nodes[in_k] @ We[ek] + be[ek])
            v = ew[c, 2] * (nodes[in_v] @ We[ev] + be[ev])
            o = _mha(q, k, v, Wq[c], Wk[c], Wv[c], Wo[c])
            nodes[c] = act_w[c] * o + q
            lind += nsrc
        out = nodes[NUM_NOD - 1]
        return _layernorm(out, ln_g, ln_b)
    x = L0_attn_x
    x = x + _L0_attn_ref(_layernorm(x, axis=-1), L0_attn_mask, L0_attn_W_qk, L0_attn_W_v, L0_attn_W_out, L0_attn_b_out, L0_attn_conv)
    x = x + _L0_ffn_ref(_layernorm(x, axis=-1), L0_ffn_ew, L0_ffn_act_w, L0_ffn_We, L0_ffn_be, L0_ffn_Wq, L0_ffn_Wk, L0_ffn_Wv, L0_ffn_Wo, L0_ffn_ln_g, L0_ffn_ln_b)
    return x

_drawn_inputs = setup_inputs


def setup_inputs(seed=0):
    import zlib

    import numpy as np

    out = dict(_drawn_inputs(seed))
    spreads = {'L0_attn_b_out': (0.0, 0.1),
     'L0_ffn_be': (0.0, 0.1),
     'L0_ffn_ln_g': (1.0, 0.2),
     'L0_ffn_ln_b': (0.0, 0.1)}
    factors = {'L0_attn_conv': 64.0, 'L0_ffn_Wq': 64.0, 'L0_ffn_Wk': 64.0}
    for name, (base, spread) in spreads.items():
        noise = np.random.default_rng([zlib.crc32(name.encode()), seed]).standard_normal(out[name].shape)
        drawn = base * np.exp(spread * noise) if base else spread * noise
        out[name] = jnp.asarray(drawn.astype(out[name].dtype))
    for name, factor in factors.items():
        out[name] = (out[name] * factor).astype(out[name].dtype)
    return out
```

```python
from contextlib import ExitStack

import numpy as np

import concourse.bass as bass
from concourse import mybir

F32 = mybir.dt.float32
F32R = mybir.dt.float32r
BF16 = mybir.dt.bfloat16
ACT = mybir.ActivationFunctionType
ALU = mybir.AluOpType
AX = mybir.AxisListType

P = 128
BATCH, TOK, DIM = 4, 1024, 128
HEADS, QUAD, DV = 8, 4, 16
SLOT = 32
CHUNK = 512
NCHUNK = TOK // CHUNK
KB = TOK // P
BPC = CHUNK // P

DQK = 64
MAXPOS = 10
NREL = 2 * MAXPOS + 1
SCALE_A = DQK ** -0.5
KROWS_A = 96
MROW_A = DQK
WIN = 2 * P + MAXPOS
EPS_X = 1e-5
EPS_G = 1e-6
NE = 512
HALF_STEPS = NCHUNK * KB
PIECES = QUAD * KB

NODES = 6
UNITS = NODES * BATCH
SCALE_B = DV ** -0.5
TERMS = ((0, 0), (0, 1), (1, 0), (1, 1), (0, 2), (2, 0))
MROW_B = DV * len(TERMS)
KROWS_B = MROW_B + 3
UNIT_STEPS = 2 * HALF_STEPS
PAIRS = (UNITS - 4) // 2
WP_COLS = 2 * P + 2
WF_COLS = 3 * P + 1

D16 = 16


def edges():
    at, out = 0, []
    for c in range(NODES):
        n = min(c + 1, 5)
        out.append((at + n - 1, at, at + n // 2))
        at += n
    return out


def side(kb, qc):
    r = kb - BPC * qc
    if r in (0, 1):
        return 0, 0, P * (r + 1) + MAXPOS, P - P * r
    if r in (2, 3):
        return 1, P * r - MAXPOS, CHUNK, 0
    if r == BPC:
        return 1, CHUNK - MAXPOS, CHUNK, 0
    if r == -1:
        return 0, 0, MAXPOS, 2 * P
    return (0 if r < 0 else 1), 0, 0, 0


def chain(eng, sem, base):
    n = [0]

    def link(ins):
        n[0] += 1
        ins.then_inc(sem, 1)
        eng.wait_ge(sem, base + n[0])
    return link


def program(nc, x, w_qk, w_v, w_out, b_out, conv, conv_rev, ew, act_w, We, be, Wq, Wk, Wv, Wo, ln_g, ln_b,
            ident, exchange, out):
    def dram(name, shape):
        return nc.dram_tensor(name, shape, F32, kind="Internal").ap()

    xnt = dram("xnt", [BATCH, P, TOK])
    x1d = dram("x1d", [BATCH * NCHUNK, P, BPC, DIM])
    node = dram("node", [UNITS + BATCH, P, TOK])
    ext = dram("ext", [4, HEADS, NE])
    wpd = dram("wpd", [NODES, P, WP_COLS])
    wvd = dram("wvd", [NODES, P, P])
    wfd = dram("wfd", [NODES, P, WF_COLS])
    partd = nc.dram_tensor("partd", [P, 2, 3, TOK], BF16, kind="Internal").ap()
    x_rows = x.rearrange("b (t p) d -> b p t d", p=P)
    out_rows = out.rearrange("b (t p) d -> b p t d", p=P)

    with ExitStack() as ctx:
        def psum(name, n):
            return ctx.enter_context(nc.psum_tensor(name, [P, n], F32))

        psM = [psum(f"ps_max{i}", TOK) for i in range(2)]
        psS = [psum(f"ps_score{i}", CHUNK) for i in range(2)]
        psO = psum("ps_ctx", CHUNK)
        psX = psum("ps_misc", CHUNK)
        sid = ctx.enter_context(nc.sbuf_tensor("ident_sb", [P, P], F32))
        stored = ctx.enter_context(nc.semaphore("node_stored"))

        with nc.sbuf_tensor("tab_scores", [P, 2, HEADS, WIN], F32) as tabS, \
                nc.sbuf_tensor("tab_maxima", [P, 2, HEADS, WIN], F32R) as tabM:
            prelude(nc, psM, psS, psX, sid, exchange, x_rows, conv, conv_rev, ew, act_w, We, be, Wq, Wk, Wv, Wo, ident,
                    xnt, ext, wpd, wvd, wfd, tabS, tabM)
            first_attention(nc, psM, psS, psO, psX, sid, x_rows, w_qk, w_v, w_out, b_out, conv, xnt, x1d, node,
                            tabS, tabM, stored)
        graph(nc, psM, psS, psO, psX, sid, wpd, wvd, wfd, node, partd, stored)
        finish(nc, psM, sid, node, x1d, ln_g, ln_b, out_rows)


def allocators(nc, ctx):
    def sb(name, shape, dt=F32):
        return ctx.enter_context(nc.sbuf_tensor(name, shape, dt))

    def sem(name):
        return ctx.enter_context(nc.semaphore(name))
    return sb, sem


def prelude(nc, psM, psS, psX, sid, exchange, x_rows, conv, conv_rev, ew, act_w, We, be, Wq, Wk, Wv, Wo, ident,
            xnt, ext, wpd, wvd, wfd, tabS, tabM):
    EDGES = edges()
    with ExitStack() as ctx:
        sb, sem = allocators(nc, ctx)
        xs = sb("xs", [P, 2, KB, DIM])
        xn = sb("xn", [P, KB, DIM])
        stats = sb("stats", [P, KB, 6])
        mv = sb("mv", [P, KB, 2])
        sd = sb("sd", [P, KB])
        rs = sb("rs", [P, KB])
        xt = sb("xt", [P, TOK])
        cv = sb("cv", [HEADS, 2, NREL])
        dv_ = sb("ext_plain", [HEADS, 2, NE])
        de = sb("ext_all", [HEADS, 4, NE])
        ewb = sb("ewb", [P, NODES * 3])
        awb = sb("awb", [P, NODES])
        ber = sb("ber", [3 * NODES, DIM])
        bet = sb("bet", [P, 3 * NODES])
        wein = sb("wein", [P, NODES, 3, P])
        wnin = sb("wnin", [P, NODES, 4, P])
        wopad = sb("wopad", [P, NODES, 2, P])
        wet = sb("wet", [P, 3, P])
        bsum = sb("bsum", [P, 2])
        bcol = sb("bcol", [P, 2])
        wps = sb("wps", [P, NODES, WP_COLS])
        wvs = sb("wvs", [P, NODES, P])
        wfs = sb("wfs", [P, NODES, WF_COLS])
        tabf = sb("tabf", [P, 4, HEADS, WIN])
        exch = sb("exch", [P, P])

        x_in = [sem("x_in0"), sem("x_in1")]
        w_in, wo_in, small_in, id_in = sem("w_in"), sem("wo_in"), sem("small_in"), sem("id_in")
        zeroed, ext_ready, ext_out, w_out_s = sem("zeroed"), sem("ext_ready"), sem("ext_out"), sem("w_out_s")
        ve_ready, sd_ready, xn_ready, xt_ready, xt_copied, xt_out = (
            sem("ve_ready"), sem("sd_ready"), sem("xn_ready"), sem("xt_ready"), sem("xt_copied"), sem("xt_out"))
        bias_chain, w_chain, tab_in = sem("bias_chain"), sem("w_chain"), sem("tab_in")
        tab_ready, tab_copied = sem("tab_ready"), sem("tab_copied")
        stats_done, aggr_done, rs_done = sem("stats_done"), sem("aggr_done"), sem("rs_done")
        be_ready, be_copied = sem("be_ready"), sem("be_copied")
        wt_ready, wt_copied, wm_ready, wm_copied, wb_ready, wb_copied, wo_ready, w_done = (
            sem("wt_ready"), sem("wt_copied"), sem("wm_ready"), sem("wm_copied"), sem("wb_ready"),
            sem("wb_copied"), sem("wo_ready"), sem("w_done"))

        with nc.Block() as block:
            @block.sync
            def _(sp):
                sp.dma_start(sid[:], ident).then_inc(id_in, D16)
                sp.dma_start(exch[:], exchange).then_inc(id_in, D16)
                for b in range(2):
                    sp.dma_start(xs[:, b], x_rows[b]).then_inc(x_in[b], D16)
                sp.dma_start(cv[:, 0], conv_rev).then_inc(small_in, D16)
                sp.dma_start(cv[:, 1], conv).then_inc(small_in, D16)
                sp.dma_start(ewb[:], ew.rearrange("n k -> (n k)").rearrange("(o n) -> o n", o=1)
                             .to_broadcast([P, NODES * 3])).then_inc(small_in, D16)
                sp.dma_start(awb[:], act_w.rearrange("(o n) -> o n", o=1)
                             .to_broadcast([P, NODES])).then_inc(small_in, D16)
                for c, e in enumerate(EDGES):
                    for k in range(3):
                        sp.dma_start(ber[3 * c + k:3 * c + k + 1, :], be[e[k]:e[k] + 1, :]).then_inc(small_in, D16)
                        sp.dma_start(wein[:, c, k], We[e[k]]).then_inc(w_in, D16)
                    for k, w in enumerate((Wq, Wk, Wv, Wo)):
                        sp.dma_start(wnin[:, c, k], w[c]).then_inc(w_in, D16)
                sp.wait_ge(zeroed, 1)
                for q in range(2):
                    for i in range(QUAD):
                        rows = Wo[:, (QUAD * q + i) * DV:(QUAD * q + i + 1) * DV, :]
                        sp.dma_start(wopad[SLOT * i:SLOT * i + DV, :, q, :],
                                     rows.rearrange("c d n -> d c n")).then_inc(wo_in, D16)
                for b in range(2, BATCH):
                    sp.wait_ge(xn_ready, b - 1)
                    sp.dma_start(xs[:, b % 2], x_rows[b]).then_inc(x_in[b % 2], D16)
                sp.wait_ge(ext_ready, 1)
                sp.dma_start(ext.rearrange("k h n -> h k n"), de[:]).then_inc(ext_out, D16)
                sp.wait_ge(ext_out, D16)
                for k in range(4):
                    first = NE // 2 - (P, MAXPOS)[k % 2] - (P - 1)
                    sp.dma_start(tabf[:, k], bass.AP(ext.tensor, k * HEADS * NE + first, [[1, P], [NE, HEADS], [1, WIN]])
                                 ).then_inc(tab_in, D16)
                sp.wait_ge(w_done, 1)
                sp.dma_start(wpd.rearrange("c p n -> p c n"), wps[:]).then_inc(w_out_s, D16)
                sp.dma_start(wvd.rearrange("c p n -> p c n"), wvs[:]).then_inc(w_out_s, D16)
                sp.dma_start(wfd.rearrange("c p n -> p c n"), wfs[:]).then_inc(w_out_s, D16)
                sp.wait_ge(w_out_s, 3 * D16)

            @block.gpsimd
            def _(pool):
                nc.gpsimd.memset(wopad[:], 0.0).then_inc(zeroed, 1)

            @block.tensor
            def _(pe):
                pe.wait_ge(id_in, 2 * D16)
                for b in range(BATCH):
                    pe.wait_ge(xn_ready, b + 1)
                    if b:
                        pe.wait_ge(xt_copied, b)
                    for t in range(KB):
                        ins = pe.transpose(psM[0][:, P * t:P * t + P], xn[:, t], sid[:])
                    ins.then_inc(xt_ready, 1)
                pe.wait_ge(small_in, (4 + 3 * NODES) * D16)
                pe.transpose(psX[:, 0:3 * NODES], ber[:], sid[0:3 * NODES, 0:3 * NODES]).then_inc(be_ready, 1)
                pe.wait_ge(w_in, 7 * NODES * D16)
                for c in range(NODES):
                    if c:
                        pe.wait_ge(wt_copied, c)
                    for k in range(3):
                        ins = pe.transpose(psM[1][:, P * k:P * k + P], wein[:, c, k], sid[:])
                    ins.then_inc(wt_ready, 1)
                    pe.wait_ge(wt_copied, c + 1)
                    pe.wait_ge(be_copied, 1)
                    for k in range(3):
                        if c and not k:
                            pe.wait_ge(wm_copied, c)
                        ins = pe.matmul(psM[1][:, CHUNK + P * k:CHUNK + P * k + P], wet[:, k], wnin[:, c, k],
                                        start=True, stop=True)
                    ins.then_inc(wm_ready, 1)
                    if c:
                        pe.wait_ge(wo_ready, c)
                    for k in range(3):
                        ins = pe.matmul(psX[:, 32 + k:33 + k], wnin[:, c, k], bet[:, 3 * c + k:3 * c + k + 1],
                                        start=True, stop=True)
                    ins.then_inc(wb_ready, 1)
                    pe.wait_ge(wb_copied, c + 1)
                    pe.matmul(psX[:, 36:37], wnin[:, c, 3], bcol[:, 0:1], start=True, stop=True).then_inc(wb_ready, 1)
                pe.wait_ge(tab_in, 4 * D16)
                for n in range(4 * HEADS):
                    if n >= 2:
                        pe.wait_ge(tab_copied, n - 1)
                    pe.matmul(psS[n % 2][:, 0:WIN], exch[:], tabf[:, n // HEADS, n % HEADS], start=True,
                              stop=True).then_inc(tab_ready, 1)

            @block.scalar
            def _(act):
                for b in range(BATCH):
                    act.wait_ge(ve_ready, b + 1)
                    act.activation(sd[:], mv[:, :, 1], ACT.Sqrt).then_inc(sd_ready, 1)
                    act.wait_ge(xt_ready, b + 1)
                    if b:
                        act.wait_ge(xt_out, b * D16)
                    act.activation(xt[:], psM[0][:], ACT.Identity).then_inc(xt_copied, 1)
                    act.wait_ge(xt_copied, b + 1)
                    act.dma_start(xnt[b], xt[:]).then_inc(xt_out, D16)
                act.wait_ge(xt_out, BATCH * D16)

            @block.vector
            def _(dve):
                dve.wait_ge(small_in, (4 + 3 * NODES) * D16)
                link = chain(dve, bias_chain, 0)
                link(nc.vector.memset(dv_[:], 0.0))
                mid = NE // 2 - MAXPOS
                for k in range(2):
                    for lo, hi, at in ((0, mid, 0), (mid + NREL, NE, NREL - 1)):
                        link(nc.vector.tensor_scalar(dv_[:, k, lo:hi], dv_[:, k, lo:hi], cv[:, k, at:at + 1], None,
                                                     ALU.add))
                    link(nc.vector.tensor_copy(dv_[:, k, mid:mid + NREL], cv[:, k, :]))
                    for s, at in ((0, NREL - 1), (1, 0)):
                        ins = nc.vector.tensor_scalar(de[:, 2 * k + s], dv_[:, k], cv[:, k, at:at + 1],
                                                      1.0 / SCALE_A, ALU.subtract, ALU.mult)
                ins.then_inc(ext_ready, 1)

                for b in range(BATCH):
                    dve.wait_ge(x_in[b % 2], (b // 2 + 1) * D16)
                    for t in range(KB):
                        ins = nc.vector.bn_stats(stats[:, t], xs[:, b % 2, t])
                    ins.then_inc(stats_done, 1)
                    dve.wait_ge(stats_done, b + 1)
                    for t in range(KB):
                        ins = nc.vector.bn_aggr(mv[:, t], stats[:, t])
                    ins.then_inc(aggr_done, 1)
                    dve.wait_ge(aggr_done, b + 1)
                    nc.vector.tensor_scalar(mv[:, :, 1], mv[:, :, 1], EPS_X, None, ALU.add).then_inc(ve_ready, 1)
                    dve.wait_ge(sd_ready, b + 1)
                    nc.vector.reciprocal(rs[:], sd[:]).then_inc(rs_done, 1)
                    dve.wait_ge(rs_done, b + 1)
                    if b:
                        dve.wait_ge(xt_ready, b)
                    for t in range(KB):
                        ins = nc.vector.tensor_scalar(xn[:, t], xs[:, b % 2, t], mv[:, t, 0:1], rs[:, t:t + 1],
                                                      ALU.subtract, ALU.mult)
                    ins.then_inc(xn_ready, 1)

                dve.wait_ge(be_ready, 1)
                nc.vector.tensor_copy(bet[:], psX[:, 0:3 * NODES]).then_inc(be_copied, 1)
                dve.wait_ge(wo_in, 2 * QUAD * D16)
                for c in range(NODES):
                    s = [ewb[:, 3 * c + k:3 * c + k + 1] for k in range(3)]
                    aw = awb[:, c:c + 1]
                    link = chain(dve, w_chain, 2 * c)
                    dve.wait_ge(wt_ready, c + 1)
                    if c:
                        dve.wait_ge(wm_ready, c)
                    nc.vector.tensor_copy(wet[:], psM[1][:, 0:3 * P].rearrange("p (k n) -> p k n", k=3)).then_inc(wt_copied, 1)
                    dve.wait_ge(wm_ready, c + 1)
                    prod_ps = psM[1][:, CHUNK:CHUNK + 3 * P].rearrange("p (k n) -> p k n", k=3)
                    for k in range(2):
                        nc.vector.tensor_scalar(wps[:, c, P * k:P * k + P], prod_ps[:, k], s[k], None, ALU.mult)
                    nc.vector.tensor_scalar(wvs[:, c], prod_ps[:, 2], s[2], None, ALU.mult).then_inc(wm_copied, 1)
                    dve.wait_ge(wb_ready, 2 * c + 1)
                    for k in range(2):
                        nc.vector.tensor_scalar(wps[:, c, 2 * P + k:2 * P + k + 1], psX[:, 32 + k:33 + k], s[k], None,
                                                ALU.mult)
                    nc.vector.tensor_scalar(bcol[:, 0:1], psX[:, 34:35], s[2], None, ALU.mult).then_inc(wb_copied, 1)
                    nc.vector.tensor_scalar(wfs[:, c, 0:P], wein[:, c, 0], s[0], None, ALU.mult)
                    nc.vector.tensor_scalar(wfs[:, c, P:3 * P], wopad[:, c].rearrange("p q n -> p (q n)"), aw, None,
                                            ALU.mult)
                    link(nc.vector.tensor_scalar(bsum[:, 0:1], bet[:, 3 * c:3 * c + 1], s[0], None, ALU.mult))
                    dve.wait_ge(wb_ready, 2 * c + 2)
                    link(nc.vector.tensor_scalar(bsum[:, 1:2], psX[:, 36:37], aw, None, ALU.mult))
                    nc.vector.tensor_tensor(wfs[:, c, 3 * P:3 * P + 1], bsum[:, 0:1], bsum[:, 1:2],
                                            ALU.add).then_inc(wo_ready, 1)
                for n in range(4 * HEADS):
                    dve.wait_ge(tab_ready, n + 1)
                    dst = tabS[:, n // HEADS, n % HEADS] if n < 2 * HEADS else tabM[:, n // HEADS - 2, n % HEADS]
                    nc.vector.tensor_copy(dst, psS[n % 2][:, 0:WIN]).then_inc(tab_copied, 1)
                nc.vector.memset(bsum[:], 0.0).then_inc(w_done, 1)


def context_done(nc, dve, c32, den, inv, g, ring, o_copied, den_step, steady):
    copied, base = known(dve, g + 1), known(dve, 2 * g)
    dve.wait_ge(steady, 1)
    dve.wait_ge(o_copied, copied)
    link = chain(dve, den_step, base)
    link(nc.vector.transpose(den[:], c32[:, ring]))
    nc.vector.reciprocal(inv[:], den[:].rearrange("p (k r) -> p k r", r=SLOT)[:, :, DV]).then_inc(den_step, 1)


def context_inverse(nc, dve, rec, inv, g, cn_done, rec_ready, den_step, steady):
    there = known(dve, 2 * g + 2)
    if not (isinstance(g, int) and g == 0):
        used = known(dve, g)
    dve.wait_ge(steady, 1)
    dve.wait_ge(den_step, there)
    if not (isinstance(g, int) and g == 0):
        dve.wait_ge(cn_done, used)
    nc.vector.transpose(rec[:], inv[:].unsqueeze(2).to_broadcast([P, CHUNK // SLOT, SLOT])).then_inc(rec_ready, 1)


def first_attention(nc, psM, psS, psO, psX, sid, x_rows, w_qk, w_v, w_out, b_out, conv, xnt, x1d, node, tabS, tabM,
                    stored):
    with ExitStack() as ctx:
        sb, sem = allocators(nc, ctx)
        khl = [sb(f"khl_{q}", [P, QUAD, TOK], F32R) for q in range(2)]
        qhh = [sb(f"qhh_{q}", [P, QUAD, TOK], F32R) for q in range(2)]
        qlm = [sb(f"qlm_{q}", [KROWS_A, QUAD, TOK], F32R) for q in range(2)]
        khm = sb("khm", [KROWS_A, QUAD, TOK], F32R)
        vs = [sb(f"vs_{q}", [P, KB, QUAD, SLOT]) for q in range(2)]
        pt = sb("pt", [P, 2, QUAD, CHUNK])
        idr = sb("idr", [P, P], F32R)
        xnb = sb("xnb", [P, TOK])
        wqk = sb("wqk", [P, 2 * HEADS * DQK])
        wv = sb("wv_a", [P, P])
        wo = sb("wo_a", [P, 2, P])
        cb = sb("cb", [P, HEADS, NREL])
        cm = sb("cm", [P, HEADS, KB, NCHUNK])
        mx2 = sb("mx2", [P, PIECES, NCHUNK])
        mx3 = sb("mx3", [P, PIECES, NCHUNK])
        mx = sb("mx_a", [P, PIECES])
        mhl = sb("mhl", [PIECES, 2, P], F32R)
        c32 = sb("c32_a", [P, 2, CHUNK])
        den = sb("den_a", [P, CHUNK])
        inv = sb("inv_a", [P, CHUNK // SLOT])
        rec = sb("rec_a", [P, CHUNK])
        cn = sb("cn_a", [P, 2, NCHUNK, CHUNK])
        bo = sb("bo", [P, DIM])
        x1 = sb("x1", [P, BPC, DIM])
        stats = sb("stats_a", [P, BPC, 6])
        mv = sb("mv_a", [P, BPC, 2])
        sd = sb("sd_a", [P, BPC])
        rs = sb("rs_a", [P, BPC])
        xh = sb("xh", [P, BPC, DIM])
        nt = sb("nt", [P, CHUNK])

        w_in, zeroed, cb_in = sem("a_w_in"), sem("a_zeroed"), sem("a_cb_in")
        consts = sem("a_consts")
        xn_in, xr_in = sem("a_xn_in"), sem("a_xr_in")
        pj_ready, pj_high, pj_low, q_twice, k_again = (
            sem("a_pj_ready"), sem("a_pj_high"), sem("a_pj_low"), sem("a_q_twice"), sem("a_k_again"))
        v_ready, v_copied = sem("a_v_ready"), sem("a_v_copied")
        mx_ready, mx_done, mx_biased, mx_final = sem("a_mx_ready"), sem("a_mx_done"), sem("a_mx_biased"), sem("a_mx_final")
        mt_ready, mt_high, mt_copied, mrow = sem("a_mt_ready"), sem("a_mt_high"), sem("a_mt_copied"), sem("a_mrow")
        s_ready, exp_done, pv_done = sem("a_s_ready"), sem("a_exp_done"), sem("a_pv_done")
        o_copied, den_step, rec_ready, cn_done = sem("a_o_copied"), sem("a_den_step"), sem("a_rec_ready"), sem("a_cn_done")
        fo_ready, fo_copied, x1_ready, x1_out = sem("a_fo_ready"), sem("a_fo_copied"), sem("a_x1_ready"), sem("a_x1_out")
        ve_ready, sd_ready, xh_ready = sem("a_ve_ready"), sem("a_sd_ready"), sem("a_xh_ready")
        stats_done, aggr_done, rs_done = sem("a_stats_done"), sem("a_aggr_done"), sem("a_rs_done")
        ft_ready, ft_copied = sem("a_ft_ready"), sem("a_ft_copied")

        PJ = 8
        PJ_ORDER = [(qk, j, c) for j in range(2) for qk in range(2) for c in range(NCHUNK)]
        TWICE_STEP = {2: 0, 3: 1, 5: 4, 6: 5}
        Q_PJ = [n for n in range(PJ) if not PJ_ORDER[n][0]]
        V_STEP, MT_STEP, FIRST_M, M_STEPS = 4, 14, 4, 10
        FO = {0: 5, 1: 10}
        FT = {0: 8, 1: 13}

        def pieces_at(s):
            first, last = (min(max(0, n), M_STEPS) for n in (s - FIRST_M, s - FIRST_M + 1))
            return range(PIECES * first // M_STEPS, PIECES * last // M_STEPS)

        def pj_bank(n):
            return psM[n % 4 // 2][:, CHUNK * (n % 2):CHUNK * (n % 2) + CHUNK]

        with nc.Block() as block:
            @block.sync
            def _(sp):
                sp.dma_start(xnb[:], xnt[0]).then_inc(xn_in, D16)
                sp.dma_start(wqk[:], w_qk).then_inc(w_in, D16)
                sp.dma_start(wv[:], w_v).then_inc(w_in, D16)
                sp.dma_start(cb[:].rearrange("p h r -> p (h r)"),
                             conv.rearrange("h r -> (h r)").rearrange("(o n) -> o n", o=1)
                             .to_broadcast([P, HEADS * NREL])).then_inc(cb_in, D16)
                sp.dma_start(bo[:], b_out.rearrange("(o n) -> o n", o=1).to_broadcast([P, DIM])).then_inc(w_in, D16)
                sp.wait_ge(zeroed, 1)
                for q in range(2):
                    for i in range(QUAD):
                        h = QUAD * q + i
                        sp.dma_start(wo[SLOT * i:SLOT * i + DV, q], w_out[h * DV:(h + 1) * DV, :]).then_inc(w_in, D16)

                def maxima(hh, q):
                    sp.wait_ge(mt_copied, hh + 1)
                    for k in range(2):
                        row = qlm[q][MROW_A + k:MROW_A + k + 1, :, :].bitcast(F32)
                        sp.dma_start(row.rearrange("o i (t n) -> o (i t) n", t=KB), mhl[:, k].bitcast(F32)).then_inc(mrow, D16)

                def x1_store(b, c):
                    f = NCHUNK * b + c
                    sp.wait_ge(x1_ready, f + 1)
                    sp.dma_start(x1d[one(f)].rearrange("o p t d -> (o p) t d"), x1[:]).then_inc(x1_out, D16)

                def node_store(b, c):
                    f = NCHUNK * b + c
                    sp.wait_ge(ft_copied, f + 1)
                    sp.dma_start(node[one(b), :, CHUNK * c:CHUNK * c + CHUNK].rearrange("o p n -> (o p) n"),
                                 nt[:]).then_inc(stored, D16)

                def load_rows(b, c):
                    f = NCHUNK * b + c
                    if not (isinstance(f, int) and f == 0):
                        sp.wait_ge(x1_out, f * D16)
                    sp.dma_start(x1[:], x_rows[one(b), :, BPC * c:BPC * c + BPC].rearrange("o p t d -> (o p) t d")
                                 ).then_inc(xr_in, D16)

                def batch(b, first, last):
                    if not first:
                        x1_store(b - 1, 1)
                    if not last:
                        sp.wait_ge(v_ready, 2 * b + 2)
                        sp.dma_start(xnb[:], xnt[one(b + 1)].rearrange("o p n -> (o p) n")).then_inc(xn_in, D16)
                    if not first:
                        node_store(b - 1, 1)
                    load_rows(b, 0)
                    maxima(2 * b + 1, 1)
                    x1_store(b, 0)
                    node_store(b, 0)
                    load_rows(b, 1)
                    if not last:
                        maxima(2 * b + 2, 0)

                maxima(0, 0)
                batch(0, True, False)
                with sp.Fori(1, BATCH - 1) as b:
                    batch(b, False, False)
                batch(BATCH - 1, False, True)
                x1_store(BATCH - 1, 1)
                node_store(BATCH - 1, 1)
                sp.wait_ge(x1_out, BATCH * NCHUNK * D16)
                sp.wait_ge(stored, BATCH * NCHUNK * D16)

            @block.tensor
            def _(pe):
                def project(hh, q, n):
                    qk, j, c = PJ_ORDER[n]
                    if q == 0 and n == 0:
                        pe.wait_ge(xn_in, (hh // 2 + 1) * D16)
                    if n >= 4:
                        pe.wait_ge(pj_low, PJ * hh + n - 3)
                    elif n == 0 and not (isinstance(hh, int) and hh == 0):
                        pe.wait_ge(mx_done, PIECES * hh)
                    col = qk * HEADS * DQK + (QUAD * q + 2 * j) * DQK
                    pe.matmul(pj_bank(n), wqk[:, col:col + P], xnb[:, CHUNK * c:CHUNK * c + CHUNK],
                              start=True, stop=True).then_inc(pj_ready, 1)

                def values(hh, q):
                    for kb in range(KB):
                        ins = pe.matmul(psX[:, 64 * kb:64 * kb + 64], xnb[:, P * kb:P * kb + P],
                                        wv[:, 64 * q:64 * q + 64], start=True, stop=True)
                    ins.then_inc(v_ready, 1)

                def maxima(hh, q, p):
                    i, qb = p // KB, p % KB
                    if p < 2:
                        pe.wait_ge(pj_low, PJ * hh + PJ - 2 + 2 * p)
                    if p % (2 * KB) == 0:
                        pe.wait_ge(q_twice, 4 * hh + 2 * (p // (2 * KB) + 1))
                    if not (isinstance(hh, int) and hh == 0 and p < 2):
                        pe.wait_ge(mx_done, PIECES * hh + p - 1)
                    for kc in range(NCHUNK):
                        s, lo, hi, at = side(qb, kc)
                        ins = pe.matmul(psM[p % 2][:, CHUNK * kc:CHUNK * kc + CHUNK], qhh[q][:, i, P * qb:P * qb + P],
                                        khl[q][:, i, CHUNK * kc:CHUNK * kc + CHUNK], start=True, stop=hi == 0)
                        if hi:
                            ins = pe.matmul(psM[p % 2][:, CHUNK * kc + lo:CHUNK * kc + hi], idr[:],
                                            tabM[:, s, QUAD * q + i, at:at + hi - lo], start=False, stop=True)
                    ins.then_inc(mx_ready, 1)

                def turn_maxima(hh):
                    pe.wait_ge(mx_final, hh + 1)
                    pe.transpose(psX[0:PIECES, 0:P], mx[:], sid[:]).then_inc(mt_ready, 1)

                def scores(hh, q, s, i):
                    n = QUAD * s + i
                    if n == 0:
                        pe.wait_ge(mrow, 2 * (hh + 1) * D16)
                    if not (isinstance(hh, int) and hh == 0 and n < 2):
                        pe.wait_ge(exp_done, QUAD * HALF_STEPS * hh + n - 1)
                    kb, qc = s % KB, s // KB
                    if s < KB and i == 0:
                        pe.wait_ge(k_again, KB * hh + kb + 1)
                    sd_, lo, hi, at = side(kb, qc)
                    pe.matmul(psS[n % 2][:], khl[q][:, i, P * kb:P * kb + P],
                              qhh[q][:, i, CHUNK * qc:CHUNK * qc + CHUNK], start=True, stop=False)
                    ins = pe.matmul(psS[n % 2][:], khm[:, i, P * kb:P * kb + P],
                                    qlm[q][:, i, CHUNK * qc:CHUNK * qc + CHUNK], start=False, stop=hi == 0)
                    if hi:
                        ins = pe.matmul(psS[n % 2][:, lo:hi], sid[:], tabS[:, sd_, QUAD * q + i, at:at + hi - lo],
                                        start=False, stop=True)
                    ins.then_inc(s_ready, 1)

                def contexts(hh, q, s):
                    kb, g = s % KB, NCHUNK * hh + s // KB
                    if s == 0:
                        pe.wait_ge(v_copied, hh + 1)
                    pe.wait_ge(exp_done, QUAD * (HALF_STEPS * hh + s + 1))
                    if kb == 0 and not (isinstance(g, int) and g == 0):
                        pe.wait_ge(o_copied, g)
                    for i in range(QUAD):
                        ins = pe.matmul(psO[SLOT * i:SLOT * i + SLOT, :], vs[q][:, kb, i], pt[:, s % 2, i],
                                        start=kb == 0, stop=kb == KB - 1)
                    ins.then_inc(pv_done, 1)

                def output(b, c):
                    pe.wait_ge(cn_done, 2 * NCHUNK * b + NCHUNK + c + 1)
                    for t in range(BPC):
                        for q in range(2):
                            ins = pe.matmul(psX[:, P * t:P * t + P], cn[:, q, c, P * t:P * t + P], wo[:, q],
                                            start=q == 0, stop=q == 1)
                    ins.then_inc(fo_ready, 1)

                def turn_rows(b, c):
                    pe.wait_ge(xh_ready, NCHUNK * b + c + 1)
                    for t in range(BPC):
                        ins = pe.transpose(psX[:, P * t:P * t + P], xh[:, t], sid[:])
                    ins.then_inc(ft_ready, 1)

                def half(hh, b, q, first, last):
                    for s in range(HALF_STEPS):
                        scores(hh, q, s, 0)
                        scores(hh, q, s, 1)
                        if not last:
                            for p in pieces_at(s):
                                maxima(hh + 1, 1 - q, p)
                            if s < PJ // 2:
                                project(hh + 1, 1 - q, 2 * s)
                            if s == V_STEP:
                                pe.wait_ge(mt_copied, hh + 1)
                                values(hh + 1, 1 - q)
                            if s == MT_STEP:
                                if not (first and q == 0):
                                    pe.wait_ge(ft_copied, NCHUNK * b + q)
                                else:
                                    pe.wait_ge(v_copied, hh + 2)
                                turn_maxima(hh + 1)
                        if s == FO[q] and not (first and q == 0):
                            if last:
                                pe.wait_ge(mt_copied, hh + 1)
                            else:
                                pe.wait_ge(v_copied, hh + 2)
                            output(b - 1 + q, 1 - q)
                        if s == FT[q] and not (first and q == 0):
                            pe.wait_ge(fo_copied, NCHUNK * b + q)
                            turn_rows(b - 1 + q, 1 - q)
                        scores(hh, q, s, 2)
                        scores(hh, q, s, 3)
                        if not last and s < PJ // 2:
                            project(hh + 1, 1 - q, 2 * s + 1)
                        if s:
                            contexts(hh, q, s - 1)
                        elif not (first and q == 0):
                            contexts(hh - 1, 1 - q, HALF_STEPS - 1)

                pe.wait_ge(w_in, (3 + 2 * QUAD) * D16)
                pe.wait_ge(consts, 1)
                for n in range(PJ):
                    project(0, 0, n)
                values(0, 0)
                for p in range(PIECES):
                    maxima(0, 0, p)
                pe.wait_ge(v_copied, 1)
                turn_maxima(0)
                half(0, 0, 0, True, False)
                half(1, 0, 1, True, False)
                with pe.Fori(1, BATCH - 1) as b:
                    half(2 * b, b, 0, False, False)
                    half(2 * b + 1, b, 1, False, False)
                half(2 * BATCH - 2, BATCH - 1, 0, False, False)
                half(2 * BATCH - 1, BATCH - 1, 1, False, True)
                contexts(2 * BATCH - 1, 1, HALF_STEPS - 1)
                pe.wait_ge(ft_copied, NCHUNK * BATCH - 1)
                output(BATCH - 1, 1)
                pe.wait_ge(fo_copied, NCHUNK * BATCH)
                turn_rows(BATCH - 1, 1)

            @block.scalar
            def _(act):
                def high(hh, q, n):
                    qk, j, c = PJ_ORDER[n]
                    act.wait_ge(pj_ready, PJ * hh + n + 1)
                    for k in range(2):
                        ins = act.activation((qhh, khl)[qk][q][0:DQK, 2 * j + k, CHUNK * c:CHUNK * c + CHUNK],
                                             pj_bank(n)[DQK * k:DQK * k + DQK, :], ACT.Identity)
                    ins.then_inc(pj_high, 1)

                def twice(hh, q, n):
                    j, c = PJ_ORDER[n][1:]
                    heads, cols = slice(2 * j, 2 * j + 2), slice(CHUNK * c, CHUNK * c + CHUNK)
                    act.wait_ge(pj_high, PJ * hh + n + 1)
                    act.activation(qhh[q][DQK:P, heads, cols], qhh[q][0:DQK, heads, cols].bitcast(F32),
                                   ACT.Identity).then_inc(q_twice, 1)

                def values(hh, q):
                    act.wait_ge(v_ready, hh + 1)
                    act.activation(vs[q][:, :, :, 0:DV], psX[:].rearrange("p (k i d) -> p k i d", k=KB, i=QUAD),
                                   ACT.Identity).then_inc(v_copied, 1)

                def root(b, c):
                    act.wait_ge(ve_ready, NCHUNK * b + c + 1)
                    act.activation(sd[:], mv[:, :, 1], ACT.Sqrt).then_inc(sd_ready, 1)

                def turned(b, c):
                    f = NCHUNK * b + c
                    act.wait_ge(ft_ready, f + 1)
                    if not (isinstance(f, int) and f == 0):
                        act.wait_ge(stored, f * D16)
                    act.activation(nt[:], psX[:], ACT.Identity).then_inc(ft_copied, 1)

                def context_copy(g, ring):
                    act.wait_ge(pv_done, KB * (g + 1))
                    if not (isinstance(g, int) and g < 2):
                        act.wait_ge(cn_done, g - 1)
                    act.activation(c32[:, ring], psO[:], ACT.Identity).then_inc(o_copied, 1)

                def half(hh, b, q, first, last):
                    begin = first and q == 0
                    for s in range(HALF_STEPS):
                        if s % KB == 1 and not (begin and s == 1):
                            context_copy(NCHUNK * hh + s // KB - 1, (s // KB + 1) % 2)
                        if not (begin and s < 2):
                            act.wait_ge(pv_done, HALF_STEPS * hh + s - 1)
                        at = (0, NREL - 1)[side(s % KB, s // KB)[0]]
                        for i in range(QUAD):
                            n = QUAD * s + i
                            act.wait_ge(s_ready, QUAD * HALF_STEPS * hh + n + 1)
                            act.activation(pt[:, s % 2, i], psS[n % 2][:], ACT.Exp, scale=SCALE_A,
                                           bias=cb[:, QUAD * q + i, at:at + 1]
                                           ).then_inc(exp_done, 1)
                            if i == 1:
                                if not last and s == V_STEP:
                                    values(hh + 1, 1 - q)
                                if s == FO[q] + 1 and not begin:
                                    root(b - 1 + q, 1 - q)
                                if s == FT[q] and not begin:
                                    turned(b - 1 + q, 1 - q)
                            if i == 0 and not last and s in TWICE_STEP:
                                twice(hh + 1, 1 - q, TWICE_STEP[s])
                            if i >= 2 and not last and s < PJ // 2:
                                high(hh + 1, 1 - q, 2 * s + i - 2)

                act.wait_ge(cb_in, D16)
                act.wait_ge(consts, 1)
                for n in range(PJ):
                    high(0, 0, n)
                for n in Q_PJ:
                    twice(0, 0, n)
                values(0, 0)
                half(0, 0, 0, True, False)
                half(1, 0, 1, True, False)
                with act.Fori(1, BATCH - 1) as b:
                    half(2 * b, b, 0, False, False)
                    half(2 * b + 1, b, 1, False, False)
                half(2 * BATCH - 2, BATCH - 1, 0, False, False)
                half(2 * BATCH - 1, BATCH - 1, 1, False, True)
                context_copy(2 * NCHUNK * BATCH - 1, 1)
                root(BATCH - 1, 1)
                turned(BATCH - 1, 1)

            @block.vector
            def _(dve):
                def low(hh, q, n):
                    qk, j, c = PJ_ORDER[n]
                    cols = slice(CHUNK * c, CHUNK * c + CHUNK)
                    dst = (qlm[q][0:DQK], khl[q][DQK:P])[qk]
                    dve.wait_ge(pj_high, PJ * hh + n + 1)
                    for k in range(2):
                        ins = nc.vector.tensor_tensor(dst[:, 2 * j + k, cols], pj_bank(n)[DQK * k:DQK * k + DQK, :],
                                                      (qhh, khl)[qk][q][0:DQK, 2 * j + k, cols].bitcast(F32),
                                                      ALU.subtract)
                    ins.then_inc(pj_low, 1)

                def maxima(hh, p):
                    dve.wait_ge(mx_ready, PIECES * hh + p + 1)
                    if p == 0 and not (isinstance(hh, int) and hh == 0):
                        dve.wait_ge(mx_final, hh)
                    nc.vector.tensor_reduce(mx2[:, p], psM[p % 2][:].rearrange("p (c n) -> p c n", c=NCHUNK), AX.X,
                                            ALU.max).then_inc(mx_done, 1)

                def maxima_final(hh, q):
                    dve.wait_ge(mx_done, PIECES * (hh + 1))
                    nc.vector.tensor_tensor(mx3[:], mx2[:], cm[:, QUAD * q:QUAD * q + QUAD].rearrange(
                        "p i t c -> p (i t) c"), ALU.add).then_inc(mx_biased, 1)
                    dve.wait_ge(mx_biased, hh + 1)
                    if not (isinstance(hh, int) and hh == 0):
                        dve.wait_ge(mt_ready, hh)
                    nc.vector.tensor_reduce(mx[:], mx3[:], AX.X, ALU.max).then_inc(mx_final, 1)

                def turned_maxima(hh):
                    dve.wait_ge(mt_ready, hh + 1)
                    if not (isinstance(hh, int) and hh == 0):
                        dve.wait_ge(mrow, 2 * hh * D16)
                    nc.vector.tensor_copy(mhl[:, 0], psX[0:PIECES, 0:P]).then_inc(mt_high, 1)
                    dve.wait_ge(mt_high, hh + 1)
                    nc.vector.tensor_tensor(mhl[:, 1], psX[0:PIECES, 0:P], mhl[:, 0].bitcast(F32),
                                            ALU.subtract).then_inc(mt_copied, 1)

                def rows_out(b, c):
                    f = NCHUNK * b + c
                    dve.wait_ge(fo_ready, f + 1)
                    dve.wait_ge(xr_in, (f + 1) * D16)
                    nc.vector.tensor_tensor(x1[:], psX[:].rearrange("p (t d) -> p t d", t=BPC), x1[:],
                                            ALU.add).then_inc(fo_copied, 1)
                    dve.wait_ge(fo_copied, f + 1)
                    nc.vector.tensor_tensor(x1[:], x1[:], bo[:].unsqueeze(1).to_broadcast([P, BPC, DIM]), ALU.add).then_inc(x1_ready, 1)
                    dve.wait_ge(x1_ready, f + 1)
                    for t in range(BPC):
                        ins = nc.vector.bn_stats(stats[:, t], x1[:, t])
                    ins.then_inc(stats_done, 1)
                    dve.wait_ge(consts, 1)
                    dve.wait_ge(stats_done, f + 1)
                    for t in range(BPC):
                        ins = nc.vector.bn_aggr(mv[:, t], stats[:, t])
                    ins.then_inc(aggr_done, 1)
                    dve.wait_ge(aggr_done, f + 1)
                    nc.vector.tensor_scalar(mv[:, :, 1], mv[:, :, 1], EPS_X, None, ALU.add).then_inc(ve_ready, 1)

                def rows_norm(b, c):
                    f = NCHUNK * b + c
                    dve.wait_ge(sd_ready, f + 1)
                    nc.vector.reciprocal(rs[:], sd[:]).then_inc(rs_done, 1)
                    dve.wait_ge(rs_done, f + 1)
                    for t in range(BPC):
                        ins = nc.vector.tensor_scalar(xh[:, t], x1[:, t], mv[:, t, 0:1], rs[:, t:t + 1],
                                                      ALU.subtract, ALU.mult)
                    ins.then_inc(xh_ready, 1)

                def half(hh, b, q, first, last):
                    begin = first and q == 0
                    for s in range(HALF_STEPS):
                        if not last:
                            for p in pieces_at(s):
                                maxima(hh + 1, p)
                            if s < PJ // 2:
                                low(hh + 1, 1 - q, 2 * s)
                                low(hh + 1, 1 - q, 2 * s + 1)
                            if s == MT_STEP - 1:
                                maxima_final(hh + 1, 1 - q)
                            if s == MT_STEP:
                                turned_maxima(hh + 1)
                        if s % KB == 1 and not (begin and s == 1):
                            context_done(nc, dve, c32, den, inv, NCHUNK * hh + s // KB - 1, (s // KB + 1) % 2,
                                         o_copied, den_step, consts)
                        if s % KB == 2 and not (begin and s == 2):
                            context_inverse(nc, dve, rec, inv, NCHUNK * hh + s // KB - 1, cn_done,
                                            rec_ready, den_step, consts)
                        if s == FO[q] and not begin:
                            rows_out(b - 1 + q, 1 - q)
                        if s == FT[q] - 1 and not begin:
                            rows_norm(b - 1 + q, 1 - q)

                for q in range(2):
                    nc.vector.memset(qlm[q][DQK:KROWS_A].bitcast(F32), 0.0)
                    nc.vector.memset(vs[q][:], 1.0)
                nc.vector.memset(khm[DQK:KROWS_A].bitcast(F32), 0.0)
                nc.vector.memset(wo[:], 0.0).then_inc(zeroed, 1)
                dve.wait_ge(zeroed, 1)
                nc.vector.memset(khm[MROW_A:MROW_A + 2].bitcast(F32), -1.0)
                nc.vector.tensor_copy(idr[:], sid[:])
                dve.wait_ge(cb_in, D16)
                for t in range(KB):
                    for c in range(NCHUNK):
                        ins = nc.vector.tensor_scalar(cm[:, :, t, c], cb[:, :, (NREL - 1, 0)[side(t, c)[0]]], 1.0 / SCALE_A, None,
                                                      ALU.mult)
                ins.then_inc(consts, 1)
                for n in range(PJ):
                    low(0, 0, n)
                for p in range(PIECES):
                    maxima(0, p)
                maxima_final(0, 0)
                turned_maxima(0)
                half(0, 0, 0, True, False)
                half(1, 0, 1, True, False)
                with dve.Fori(1, BATCH - 1) as b:
                    half(2 * b, b, 0, False, False)
                    half(2 * b + 1, b, 1, False, False)
                half(2 * BATCH - 2, BATCH - 1, 0, False, False)
                half(2 * BATCH - 1, BATCH - 1, 1, False, True)
                context_done(nc, dve, c32, den, inv, 2 * NCHUNK * BATCH - 1, 1, o_copied, den_step, consts)
                context_inverse(nc, dve, rec, inv, 2 * NCHUNK * BATCH - 1, cn_done, rec_ready, den_step, consts)
                rows_out(BATCH - 1, 1)
                rows_norm(BATCH - 1, 1)

            @block.gpsimd
            def _(pool):
                def normalise(hh, q, c):
                    g = NCHUNK * hh + c
                    pool.wait_ge(rec_ready, g + 1)
                    if not (isinstance(hh, int) and hh < 2):
                        pool.wait_ge(fo_ready, hh - q - NCHUNK + c + 1)
                    nc.gpsimd.tensor_tensor(cn[:, q, c], c32[:, c], rec[:], ALU.mult).then_inc(cn_done, 1)

                def again(hh, q, kb):
                    start = isinstance(hh, int) and hh == 0
                    if start and kb == 0:
                        pool.wait_ge(pj_high, PJ)
                    if not start:
                        used = known(pool, QUAD * (HALF_STEPS * (hh - 1) + KB + kb + 1))
                        pool.wait_ge(consts, 1)
                        pool.wait_ge(s_ready, used)
                    cols = slice(P * kb, P * kb + P)
                    nc.gpsimd.tensor_scalar(khm[0:DQK, :, cols], khl[q][0:DQK, :, cols].bitcast(F32), 0.0, None, ALU.add
                                            ).then_inc(k_again, 1)

                def half(hh, q, first, last):
                    if not (first and q == 0):
                        normalise(hh - 1, 1 - q, 1)
                    if not last:
                        for kb in range(2):
                            again(hh + 1, 1 - q, kb)
                    normalise(hh, q, 0)
                    if not last:
                        for kb in range(2, KB):
                            again(hh + 1, 1 - q, kb)

                for kb in range(KB):
                    again(0, 0, kb)
                half(0, 0, True, False)
                half(1, 1, True, False)
                with pool.Fori(1, BATCH - 1) as b:
                    half(2 * b, 0, False, False)
                    half(2 * b + 1, 1, False, False)
                half(2 * BATCH - 2, 0, False, False)
                half(2 * BATCH - 1, 1, False, True)
                normalise(2 * BATCH - 1, 1, 1)


def known(eng, value):
    return value if isinstance(value, int) else eng.snap(eng.to_reg(value))


def one(i):
    return slice(i, i + 1) if isinstance(i, int) else bass.ds(i, 1)


def graph(nc, psM, psS, psO, psX, sid, wpd, wvd, wfd, node, partd, stored):
    with ExitStack() as ctx:
        sb, sem = allocators(nc, ctx)
        qs = [sb(f"qs{i}", [KROWS_B, HEADS, TOK], BF16) for i in range(2)]
        ks = [sb(f"ks{i}", [P, HEADS, TOK], BF16) for i in range(2)]
        vs = [sb(f"vs{i}", [P, KB, HEADS, SLOT]) for i in range(2)]
        pt = sb("pt_b", [P, 2, QUAD, CHUNK])
        part = sb("part", [P, 2, 3, TOK], BF16)
        full = sb("full", [P, 2, TOK])
        rest = sb("rest", [P, CHUNK])
        xq, xk, xv, xf = sb("xq", [P, TOK]), sb("xk", [P, TOK]), sb("xv", [P, TOK]), sb("xf", [P, TOK])
        wp, wv, wf = sb("wp", [P, WP_COLS]), sb("wv_b", [P, P]), sb("wf", [P, WF_COLS])
        mx = sb("mx_b", [P, 2 * PIECES])
        m32, mrest = sb("m32_b", [PIECES, P]), sb("mrest", [PIECES, P])
        mpart = sb("mpart", [PIECES, 3, P], BF16)
        c32, rec = sb("c32_b", [P, 2, CHUNK]), sb("rec_b", [P, CHUNK])
        den, inv = sb("den_b", [P, CHUNK]), sb("inv_b", [P, CHUNK // SLOT])
        cn = sb("cn_b", [P, 2, NCHUNK, CHUNK])
        nt = sb("nt_b", [P, NCHUNK, CHUNK])

        ones = sem("b_ones")
        minus = sem("b_minus")
        p_in, v_in, f_in = sem("b_p_in"), sem("b_v_in"), sem("b_f_in")
        pj_ready, pj_copied, split_done, rest_done = (
            sem("b_pj_ready"), sem("b_pj_copied"), sem("b_split_done"), sem("b_rest_done"))
        spilled = sem("b_spilled")
        stacked = [sem("b_stacked0"), sem("b_stacked1")]
        v_ready, v_copied = sem("b_v_ready"), sem("b_v_copied")
        mx_ready, mx_done = sem("b_mx_ready"), sem("b_mx_done")
        mt_ready, mt_copied, mp_step, mp_done = sem("b_mt_ready"), sem("b_mt_copied"), sem("b_mp_step"), sem("b_mp_done")
        mrow = [sem("b_mrow0"), sem("b_mrow1")]
        s_ready, exp_done, pv_done = sem("b_s_ready"), sem("b_exp_done"), sem("b_pv_done")
        o_copied, den_step, rec_ready, cn_done = sem("b_o_copied"), sem("b_den_step"), sem("b_rec_ready"), sem("b_cn_done")
        fin_ready, fin_copied = sem("b_fin_ready"), sem("b_fin_copied")

        PJ = 2 * NCHUNK
        NS = QUAD * UNIT_STEPS
        NM = 2 * PIECES
        NG = 2 * NCHUNK
        STACK = 2 * len(TERMS) * D16
        PER_STEP = NM // UNIT_STEPS
        PJ_STEP = {9: 0, 10: 1, 12: 2, 13: 3}
        V_STEP = {6: 0, 7: 1}
        MT1_STEP, FIN1_STEP, MT0_STEP, FIN0_STEP = 1, 4, 17, 28
        GROUP_STEP = {KB * g + 1: g for g in range(NG)}

        def is_first(u):
            return isinstance(u, int) and u == 0

        with nc.Block() as block:
            @block.sync
            def _(sp):
                def row(t, i):
                    return t[one(i)].rearrange("o p n -> (o p) n")

                def at(value):
                    return known(sp, value)

                def load_projection(w):
                    used, there = at(PJ * w), at(NCHUNK * D16 * (w + 1))
                    c, query_at = at(w // BATCH), at(w)
                    key_at = at(w % BATCH + w // (5 * BATCH) * BATCH)
                    if not is_first(w):
                        sp.wait_ge(pj_copied, used)
                    sp.wait_ge(stored, there)
                    sp.dma_start(wp[:], row(wpd, c)).then_inc(p_in, D16)
                    sp.dma_start(xq[:], row(node, query_at)).then_inc(p_in, D16)
                    sp.dma_start(xk[:], row(node, key_at)).then_inc(p_in, D16)

                def load_values(w):
                    used, there = at(2 * w), at(NCHUNK * D16 * (w + 1))
                    c, value_at = at(w // BATCH), at((w // BATCH + 1) // 2 * BATCH + w % BATCH)
                    if not is_first(w):
                        sp.wait_ge(v_ready, used)
                    sp.wait_ge(stored, there)
                    sp.dma_start(wv[:], row(wvd, c)).then_inc(v_in, D16)
                    sp.dma_start(xv[:], row(node, value_at)).then_inc(v_in, D16)

                def load_residual(u):
                    used, c, query_at = at(NCHUNK * u), at(u // BATCH), at(u)
                    if not is_first(u):
                        sp.wait_ge(fin_copied, used)
                    sp.dma_start(wf[:], row(wfd, c)).then_inc(f_in, D16)
                    sp.dma_start(xf[:], row(node, query_at)).then_inc(f_in, D16)

                def spill(w):
                    sp.wait_ge(split_done, PJ * (w + 1))
                    sp.dma_start(partd, part[:]).then_inc(spilled, D16)

                def stack(w, par, q):
                    there = at(D16 * (w + 1))
                    free = at(NS * (w - 2) + NS // 2 * (q + 1))
                    if not (isinstance(w, int) and w < 2):
                        sp.wait_ge(s_ready, free)
                    sp.wait_ge(spilled, there)
                    for t, (a, b) in enumerate(TERMS):
                        for qk, dst, k in ((0, qs, a), (1, ks, b)):
                            src = partd[:, qk, k].rearrange("(h d) t -> d h t", d=DV)
                            sp.dma_start(dst[par][DV * t:DV * t + DV, QUAD * q:QUAD * q + QUAD, :],
                                         src[:, QUAD * q:QUAD * q + QUAD]).then_inc(stacked[q], D16)

                def maxima_rows(w, par, q):
                    sp.wait_ge(mp_done, 2 * w + q + 1)
                    for k in range(3):
                        dst = qs[par][MROW_B + k:MROW_B + k + 1, QUAD * q:QUAD * q + QUAD, :]
                        sp.dma_start(dst.rearrange("o i (t n) -> o (i t) n", t=KB), mpart[:, k]).then_inc(mrow[q], D16)

                def store(u, c):
                    ready, before = at(NCHUNK * u + c + 1), at(D16 * (NCHUNK * (u + BATCH) + c))
                    entry = at(u + BATCH)
                    sp.wait_ge(fin_copied, ready)
                    if not (is_first(u) and c == 0):
                        sp.wait_ge(stored, before)
                    sp.dma_start(node[one(entry), :, CHUNK * c:CHUNK * c + CHUNK].rearrange("o p n -> (o p) n"),
                                 nt[:, c]).then_inc(stored, D16)

                def unit(u, par, look):
                    if look >= 1:
                        stack(u + 1, 1 - par, 1)
                    if look >= 2:
                        load_projection(u + 2)
                    if look >= 1:
                        load_values(u + 1)
                    maxima_rows(u, par, 1)
                    if not is_first(u):
                        store(u - 1, 1)
                    load_residual(u)
                    if look >= 2:
                        spill(u + 2)
                        stack(u + 2, par, 0)
                    if look >= 1:
                        maxima_rows(u + 1, 1 - par, 0)
                    store(u, 0)

                load_projection(0)
                load_values(0)
                spill(0)
                stack(0, 0, 0)
                stack(0, 0, 1)
                load_projection(1)
                spill(1)
                stack(1, 1, 0)
                maxima_rows(0, 0, 0)
                unit(0, 0, 2)
                with sp.Fori(0, PAIRS) as i:
                    unit(2 * i + 1, 1, 2)
                    unit(2 * i + 2, 0, 2)
                unit(UNITS - 3, 1, 2)
                unit(UNITS - 2, 0, 1)
                unit(UNITS - 1, 1, 0)
                store(UNITS - 1, 1)
                sp.wait_ge(stored, (UNITS + BATCH) * NCHUNK * D16)

            @block.tensor
            def _(pe):
                def project(w, n):
                    qk, c = n // NCHUNK, n % NCHUNK
                    if n == 0:
                        pe.wait_ge(p_in, 3 * D16 * (w + 1))
                    pe.matmul(psX[:], wp[:, P * qk:P * qk + P], (xq, xk)[qk][:, CHUNK * c:CHUNK * c + CHUNK],
                              start=True, stop=True).then_inc(pj_ready, 1)

                def values(w, n):
                    if n == 0:
                        pe.wait_ge(v_in, 2 * D16 * (w + 1))
                    for t in range(BPC):
                        kb = BPC * n + t
                        ins = pe.matmul(psX[:, P * t:P * t + P], xv[:, P * kb:P * kb + P], wv[:],
                                        start=True, stop=True)
                    ins.then_inc(v_ready, 1)

                def maxima(w, par, p):
                    h, qb = p // KB, p % KB
                    if p % PIECES == 0:
                        pe.wait_ge(stacked[p // PIECES], STACK * (w + 1))
                    if not (is_first(w) and p < 2):
                        pe.wait_ge(mx_done, NM * w + p - 1)
                    for kc in range(NCHUNK):
                        ins = pe.matmul(psM[p % 2][:, CHUNK * kc:CHUNK * kc + CHUNK],
                                        qs[par][0:MROW_B, h, P * qb:P * qb + P],
                                        ks[par][0:MROW_B, h, CHUNK * kc:CHUNK * kc + CHUNK], start=True, stop=True)
                    ins.then_inc(mx_ready, 1)

                def turn_maxima(w, q):
                    pe.wait_ge(mx_done, NM * w + PIECES * (q + 1))
                    pe.transpose(psX[0:PIECES, 0:P], mx[:, PIECES * q:PIECES * q + PIECES], sid[:]).then_inc(mt_ready, 1)

                def scores(u, par, s, i):
                    n = QUAD * s + i
                    if n % (NS // 2) == 0:
                        pe.wait_ge(mrow[s // HALF_STEPS], 3 * D16 * (u + 1))
                    if not (is_first(u) and n < 2):
                        pe.wait_ge(exp_done, NS * u + n - 1)
                    h, qc, kb = QUAD * (s // HALF_STEPS) + i, s // KB % NCHUNK, s % KB
                    pe.matmul(psS[n % 2][:], ks[par][0:KROWS_B, h, P * kb:P * kb + P],
                              qs[par][0:KROWS_B, h, CHUNK * qc:CHUNK * qc + CHUNK],
                              start=True, stop=True).then_inc(s_ready, 1)

                def contexts(u, par, s):
                    kb, g = s % KB, s // KB
                    if s == 0:
                        pe.wait_ge(v_copied, 2 * (u + 1))
                    pe.wait_ge(exp_done, NS * u + QUAD * (s + 1))
                    if kb == 0 and not (is_first(u) and g == 0):
                        pe.wait_ge(o_copied, NG * u + g)
                    for i in range(QUAD):
                        ins = pe.matmul(psO[SLOT * i:SLOT * i + SLOT, :], vs[par][:, kb, QUAD * (s // HALF_STEPS) + i],
                                        pt[:, s % 2, i], start=kb == 0, stop=kb == KB - 1)
                    ins.then_inc(pv_done, 1)

                def output(u, c):
                    pe.wait_ge(f_in, 2 * D16 * (u + 1))
                    pe.wait_ge(cn_done, NG * u + NCHUNK + c + 1)
                    pe.matmul(psX[:], wf[:, 0:P], xf[:, CHUNK * c:CHUNK * c + CHUNK], start=True, stop=False)
                    pe.matmul(psX[:], wf[:, P:2 * P], cn[:, 0, c], start=False, stop=False)
                    pe.matmul(psX[:], wf[:, 2 * P:3 * P], cn[:, 1, c], start=False, stop=True).then_inc(fin_ready, 1)

                def unit(u, par, look):
                    for s in range(UNIT_STEPS):
                        scores(u, par, s, 0)
                        scores(u, par, s, 1)
                        if look >= 1:
                            for p in range(PER_STEP * s, PER_STEP * (s + 1)):
                                maxima(u + 1, 1 - par, p)
                        if s == MT1_STEP:
                            if is_first(u):
                                pe.wait_ge(mt_copied, 1)
                            else:
                                pe.wait_ge(fin_copied, NCHUNK * u - 1)
                            turn_maxima(u, 1)
                        if s == FIN1_STEP and not is_first(u):
                            pe.wait_ge(mt_copied, 2 * (u + 1))
                            output(u - 1, 1)
                        if s in V_STEP and look >= 1:
                            if V_STEP[s]:
                                pe.wait_ge(v_copied, 2 * (u + 1) + 1)
                            elif is_first(u):
                                pe.wait_ge(mt_copied, 2)
                            else:
                                pe.wait_ge(fin_copied, NCHUNK * u)
                            values(u + 1, V_STEP[s])
                        if s in PJ_STEP and look >= 2:
                            if PJ_STEP[s]:
                                pe.wait_ge(pj_copied, PJ * (u + 2) + PJ_STEP[s])
                            else:
                                pe.wait_ge(v_copied, 2 * (u + 2))
                            project(u + 2, PJ_STEP[s])
                        if s == MT0_STEP and look >= 1:
                            if look >= 2:
                                pe.wait_ge(pj_copied, PJ * (u + 3))
                            else:
                                pe.wait_ge(v_copied, 2 * (u + 2))
                            turn_maxima(u + 1, 0)
                        if s == FIN0_STEP:
                            if look >= 1:
                                pe.wait_ge(mt_copied, 2 * (u + 1) + 1)
                            else:
                                pe.wait_ge(fin_copied, NCHUNK * u)
                            output(u, 0)
                        scores(u, par, s, 2)
                        scores(u, par, s, 3)
                        if s:
                            contexts(u, par, s - 1)
                        elif not is_first(u):
                            contexts(u - 1, 1 - par, UNIT_STEPS - 1)

                for n in range(PJ):
                    if n:
                        pe.wait_ge(pj_copied, n)
                    project(0, n)
                for n in range(2):
                    if n:
                        pe.wait_ge(v_copied, n)
                    else:
                        pe.wait_ge(pj_copied, PJ)
                    values(0, n)
                pe.wait_ge(v_copied, 2)
                for n in range(PJ):
                    if n:
                        pe.wait_ge(pj_copied, PJ + n)
                    project(1, n)
                for p in range(NM):
                    maxima(0, 0, p)
                    if p == PIECES + 1:
                        pe.wait_ge(pj_copied, 2 * PJ)
                        turn_maxima(0, 0)
                pe.wait_ge(minus, 1)
                unit(0, 0, 2)
                with pe.Fori(0, PAIRS) as i:
                    unit(2 * i + 1, 1, 2)
                    unit(2 * i + 2, 0, 2)
                unit(UNITS - 3, 1, 2)
                unit(UNITS - 2, 0, 1)
                unit(UNITS - 1, 1, 0)
                contexts(UNITS - 1, 1, UNIT_STEPS - 1)
                pe.wait_ge(fin_copied, NCHUNK * UNITS - 1)
                output(UNITS - 1, 1)

            @block.scalar
            def _(act):
                def project(w, n):
                    qk, c = n // NCHUNK, n % NCHUNK
                    cols = slice(CHUNK * c, CHUNK * c + CHUNK)
                    act.wait_ge(pj_ready, PJ * w + n + 1)
                    if n == 0 and not is_first(w):
                        act.wait_ge(stacked[1], STACK * w)
                    act.activation(full[:, qk, cols], psX[:], ACT.Identity, bias=wp[:, 2 * P + qk:2 * P + qk + 1])
                    act.activation(part[:, qk, 0, cols], psX[:], ACT.Identity,
                                   bias=wp[:, 2 * P + qk:2 * P + qk + 1]).then_inc(pj_copied, 1)

                def values(w, par, n):
                    act.wait_ge(v_ready, 2 * w + n + 1)
                    act.activation(vs[par][:, BPC * n:BPC * n + BPC, :, 0:DV],
                                   psX[:].rearrange("p (k h d) -> p k h d", k=BPC, h=HEADS),
                                   ACT.Identity).then_inc(v_copied, 1)

                def turned_maxima(w, q):
                    act.wait_ge(mt_ready, 2 * w + q + 1)
                    if q:
                        act.wait_ge(mrow[0], 3 * D16 * (w + 1))
                    elif not is_first(w):
                        act.wait_ge(mrow[1], 3 * D16 * w)
                    act.activation(m32[:], psX[0:PIECES, 0:P], ACT.Identity)
                    act.activation(mpart[:, 0], psX[0:PIECES, 0:P], ACT.Identity).then_inc(mt_copied, 1)

                def output(u, c):
                    act.wait_ge(fin_ready, NCHUNK * u + c + 1)
                    if not is_first(u):
                        act.wait_ge(stored, D16 * (NCHUNK * (u - 1 + BATCH) + c + 1))
                    act.activation(nt[:, c], psX[:], ACT.Identity, bias=wf[:, 3 * P:3 * P + 1]).then_inc(fin_copied, 1)

                def context_copy(u, g):
                    act.wait_ge(pv_done, UNIT_STEPS * u + KB * (g + 1))
                    if not (is_first(u) and g < 2):
                        act.wait_ge(cn_done, NG * u + g - 1)
                    act.activation(c32[:, g % 2], psO[:], ACT.Identity).then_inc(o_copied, 1)

                def unit(u, par, look):
                    for s in range(UNIT_STEPS):
                        if s in GROUP_STEP and not (is_first(u) and s == 1):
                            if s == 1:
                                context_copy(u - 1, NG - 1)
                            else:
                                context_copy(u, GROUP_STEP[s] - 1)
                        if not (is_first(u) and s < 2):
                            act.wait_ge(pv_done, UNIT_STEPS * u + s - 1)
                        for i in range(QUAD):
                            n = QUAD * s + i
                            act.wait_ge(s_ready, NS * u + n + 1)
                            act.activation(pt[:, s % 2, i], psS[n % 2][:], ACT.Exp, scale=SCALE_B
                                           ).then_inc(exp_done, 1)
                            if i == QUAD - 1:
                                if s == MT1_STEP:
                                    turned_maxima(u, 1)
                                if s == MT0_STEP and look >= 1:
                                    turned_maxima(u + 1, 0)
                                if s == FIN1_STEP and not is_first(u):
                                    output(u - 1, 1)
                                if s in V_STEP and look >= 1:
                                    values(u + 1, 1 - par, V_STEP[s])
                                if s in PJ_STEP and look >= 2:
                                    project(u + 2, PJ_STEP[s])
                                if s == FIN0_STEP:
                                    output(u, 0)

                for n in range(PJ):
                    project(0, n)
                act.wait_ge(ones, 1)
                for n in range(2):
                    values(0, 0, n)
                for n in range(PJ):
                    project(1, n)
                turned_maxima(0, 0)
                unit(0, 0, 2)
                with act.Fori(0, PAIRS) as i:
                    unit(2 * i + 1, 1, 2)
                    unit(2 * i + 2, 0, 2)
                unit(UNITS - 3, 1, 2)
                unit(UNITS - 2, 0, 1)
                unit(UNITS - 1, 1, 0)
                context_copy(UNITS - 1, NG - 1)
                output(UNITS - 1, 1)

            @block.vector
            def _(dve):
                def maxima(w, p):
                    dve.wait_ge(mx_ready, NM * w + p + 1)
                    if p % PIECES == 0 and not is_first(w):
                        dve.wait_ge(mt_ready, 2 * w - 1 + p // PIECES)
                    nc.vector.tensor_reduce(mx[:, p:p + 1], psM[p % 2][:], AX.X, ALU.max).then_inc(mx_done, 1)

                def unit(u, par, look):
                    for s in range(UNIT_STEPS):
                        if look >= 1:
                            for p in range(PER_STEP * s, PER_STEP * (s + 1)):
                                maxima(u + 1, p)
                        if s in GROUP_STEP and not (is_first(u) and s == 1):
                            g = GROUP_STEP[s] - 1
                            context_done(nc, dve, c32, den, inv, NG * u + g, g % 2, o_copied, den_step, ones)
                        if s - 1 in GROUP_STEP and not (is_first(u) and s == 2):
                            g = GROUP_STEP[s - 1] - 1
                            context_inverse(nc, dve, rec, inv, NG * u + g, cn_done, rec_ready, den_step, ones)

                for i in range(2):
                    ins = nc.vector.memset(vs[i][:], 1.0)
                ins.then_inc(ones, 1)
                for i in range(2):
                    ins = nc.vector.memset(ks[i][MROW_B:P], -1.0)
                ins.then_inc(minus, 1)
                for p in range(NM):
                    maxima(0, p)
                unit(0, 0, 2)
                with dve.Fori(0, PAIRS) as i:
                    unit(2 * i + 1, 1, 2)
                    unit(2 * i + 2, 0, 2)
                unit(UNITS - 3, 1, 2)
                unit(UNITS - 2, 0, 1)
                unit(UNITS - 1, 1, 0)
                context_done(nc, dve, c32, den, inv, NG * UNITS - 1, 1, o_copied, den_step, ones)
                context_inverse(nc, dve, rec, inv, NG * UNITS - 1, cn_done, rec_ready, den_step, ones)

            @block.gpsimd
            def _(pool):
                def split(w, n):
                    qk, c = n // NCHUNK, n % NCHUNK
                    cols = slice(CHUNK * c, CHUNK * c + CHUNK)
                    pool.wait_ge(pj_copied, PJ * w + n + 1)
                    if not (is_first(w) and n == 0):
                        pool.wait_ge(split_done, PJ * w + n)
                    nc.gpsimd.tensor_tensor(part[:, qk, 1, cols], full[:, qk, cols], part[:, qk, 0, cols],
                                            ALU.subtract)
                    nc.gpsimd.tensor_tensor(rest[:], full[:, qk, cols], part[:, qk, 0, cols],
                                            ALU.subtract).then_inc(rest_done, 1)
                    pool.wait_ge(rest_done, PJ * w + n + 1)
                    nc.gpsimd.tensor_tensor(part[:, qk, 2, cols], rest[:], part[:, qk, 1, cols],
                                            ALU.subtract).then_inc(split_done, 1)

                def split_maxima(w, q):
                    pool.wait_ge(mt_copied, 2 * w + q + 1)
                    nc.gpsimd.tensor_tensor(mpart[:, 1], m32[:], mpart[:, 0], ALU.subtract)
                    nc.gpsimd.tensor_tensor(mrest[:], m32[:], mpart[:, 0], ALU.subtract).then_inc(mp_step, 1)
                    pool.wait_ge(mp_step, 2 * w + q + 1)
                    nc.gpsimd.tensor_tensor(mpart[:, 2], mrest[:], mpart[:, 1], ALU.subtract).then_inc(mp_done, 1)

                def normalise(u, g):
                    pool.wait_ge(rec_ready, NG * u + g + 1)
                    if not is_first(u):
                        pool.wait_ge(fin_ready, NCHUNK * (u - 1) + g % 2 + 1)
                    nc.gpsimd.tensor_tensor(cn[:, g // 2, g % 2], c32[:, g % 2], rec[:],
                                            ALU.mult).then_inc(cn_done, 1)

                def unit(u, look):
                    if not is_first(u):
                        normalise(u - 1, NG - 1)
                    split_maxima(u, 1)
                    if look >= 2:
                        split(u + 2, 0)
                    normalise(u, 0)
                    if look >= 2:
                        for n in range(1, PJ):
                            split(u + 2, n)
                    normalise(u, 1)
                    if look >= 1:
                        split_maxima(u + 1, 0)
                    normalise(u, 2)

                for w in range(2):
                    for n in range(PJ):
                        split(w, n)
                split_maxima(0, 0)
                unit(0, 2)
                with pool.Fori(0, PAIRS) as i:
                    unit(2 * i + 1, 2)
                    unit(2 * i + 2, 2)
                unit(UNITS - 3, 2)
                unit(UNITS - 2, 1)
                unit(UNITS - 1, 0)
                normalise(UNITS - 1, NG - 1)


def finish(nc, psM, sid, node, x1d, ln_g, ln_b, out_rows):
    with ExitStack() as ctx:
        sb, sem = allocators(nc, ctx)
        nin = sb("nin", [P, 2, TOK])
        x1 = sb("x1_c", [P, 2, KB, DIM])
        gb = sb("gb", [P, 2, DIM])
        yn = sb("yn", [P, KB, DIM])
        yg = sb("yg", [P, KB, DIM])
        yb = sb("yb", [P, KB, DIM])
        yo = sb("yo", [P, 2, KB, DIM])
        stats = sb("stats_c", [P, KB, 6])
        mv = sb("mv_c", [P, KB, 2])
        sd, rs = sb("sd_c", [P, KB]), sb("rs_c", [P, KB])
        n_in, x_in = [sem("c_n_in0"), sem("c_n_in1")], [sem("c_x_in0"), sem("c_x_in1")]
        gb_in, turned, ve_ready, sd_ready, scaled = (
            sem("c_gb_in"), sem("c_turned"), sem("c_ve_ready"), sem("c_sd_ready"), sem("c_scaled"))
        step, y_ready, y_out = sem("c_step"), sem("c_y_ready"), sem("c_y_out")
        LINKS = 5

        with nc.Block() as block:
            @block.sync
            def _(sp):
                for k, w in enumerate((ln_g, ln_b)):
                    sp.dma_start(gb[:, k], w.rearrange("(o n) -> o n", o=1).to_broadcast([P, DIM])).then_inc(gb_in, D16)
                for b in range(BATCH):
                    if b >= 2:
                        sp.wait_ge(y_ready, b - 1)
                    sp.dma_start(nin[:, b % 2], node[UNITS + b]).then_inc(n_in[b % 2], D16)
                    for c in range(NCHUNK):
                        sp.dma_start(x1[:, b % 2, BPC * c:BPC * c + BPC], x1d[NCHUNK * b + c]).then_inc(x_in[b % 2], D16)
                for b in range(BATCH):
                    sp.wait_ge(y_ready, b + 1)
                    sp.dma_start(out_rows[b], yo[:, b % 2]).then_inc(y_out, D16)
                    sp.wait_ge(y_out, (b + 1) * D16)

            @block.tensor
            def _(pe):
                for b in range(BATCH):
                    pe.wait_ge(n_in[b % 2], (b // 2 + 1) * D16)
                    if b >= 2:
                        pe.wait_ge(scaled, b - 1)
                    for t in range(KB):
                        ins = pe.transpose(psM[b % 2][:, P * t:P * t + P], nin[:, b % 2, P * t:P * t + P], sid[:])
                    ins.then_inc(turned, 1)

            @block.scalar
            def _(act):
                for b in range(BATCH):
                    act.wait_ge(ve_ready, b + 1)
                    act.activation(sd[:], mv[:, :, 1], ACT.Sqrt).then_inc(sd_ready, 1)

            @block.vector
            def _(dve):
                dve.wait_ge(gb_in, 2 * D16)
                for b in range(BATCH):
                    link = chain(dve, step, LINKS * b)
                    y = psM[b % 2][:].rearrange("p (t d) -> p t d", t=KB)
                    dve.wait_ge(turned, b + 1)
                    for t in range(KB):
                        ins = nc.vector.bn_stats(stats[:, t], y[:, t])
                    link(ins)
                    for t in range(KB):
                        ins = nc.vector.bn_aggr(mv[:, t], stats[:, t])
                    link(ins)
                    nc.vector.tensor_scalar(mv[:, :, 1], mv[:, :, 1], EPS_G, None, ALU.add).then_inc(ve_ready, 1)
                    dve.wait_ge(sd_ready, b + 1)
                    link(nc.vector.reciprocal(rs[:], sd[:]))
                    for t in range(KB):
                        ins = nc.vector.tensor_scalar(yn[:, t], y[:, t], mv[:, t, 0:1], rs[:, t:t + 1],
                                                      ALU.subtract, ALU.mult)
                    ins.then_inc(scaled, 1)
                    dve.wait_ge(scaled, b + 1)
                    for t in range(KB):
                        ins = nc.vector.tensor_tensor(yg[:, t], yn[:, t], gb[:, 0], ALU.mult)
                    link(ins)
                    dve.wait_ge(x_in[b % 2], NCHUNK * (b // 2 + 1) * D16)
                    if b >= 2:
                        dve.wait_ge(y_out, (b - 1) * D16)
                    for t in range(KB):
                        ins = nc.vector.tensor_tensor(yb[:, t], x1[:, b % 2, t], gb[:, 1], ALU.add)
                    link(ins)
                    nc.vector.tensor_tensor(yo[:, b % 2], yg[:], yb[:], ALU.add).then_inc(y_ready, 1)
                    dve.wait_ge(y_ready, b + 1)


_IN = ("L0_attn_x", "L0_attn_W_qk", "L0_attn_W_v", "L0_attn_W_out", "L0_attn_b_out", "L0_attn_conv", "conv_reversed",
       "L0_ffn_ew", "L0_ffn_act_w", "L0_ffn_We", "L0_ffn_be", "L0_ffn_Wq", "L0_ffn_Wk", "L0_ffn_Wv", "L0_ffn_Wo",
       "L0_ffn_ln_g", "L0_ffn_ln_b", "identity", "exchange")


def kernel(**inputs):
    import concourse.bacc as bacc
    from concourse.bass_utils import run_bass_kernel_spmd

    given = {k: np.ascontiguousarray(v) for k, v in inputs.items() if k != "L0_attn_mask"}
    given["conv_reversed"] = np.ascontiguousarray(np.asarray(inputs["L0_attn_conv"])[:, ::-1])
    given["identity"] = np.eye(P, dtype=np.float32)
    given["exchange"] = np.ascontiguousarray(given["identity"][::-1])
    nc = bacc.Bacc("TRN2", target_bir_lowering=False, num_devices=1)
    arrays, args = {}, []
    for name in _IN:
        arrays[f"in_{name}"] = given[name]
        args.append(nc.dram_tensor(f"in_{name}", given[name].shape, F32, kind="ExternalInput").ap())
    out = nc.dram_tensor("out_0", (BATCH, TOK, DIM), F32, kind="ExternalOutput").ap()
    program(nc, *args, out)
    return run_bass_kernel_spmd(nc, [arrays], core_ids=[0]).results[0]["out_0"]
```

```python
from contextlib import ExitStack

import numpy as np

import concourse.bass as bass
from concourse import mybir

F32 = mybir.dt.float32
F32R = mybir.dt.float32r
BF16 = mybir.dt.bfloat16
ACT = mybir.ActivationFunctionType
ALU = mybir.AluOpType
AX = mybir.AxisListType

P = 128
BATCH, TOK, DIM = 4, 1024, 128
HEADS, QUAD, DV = 8, 4, 16
SLOT = 32
CHUNK = 512
NCHUNK = TOK // CHUNK
KB = TOK // P
BPC = CHUNK // P

DQK = 64
MAXPOS = 10
NREL = 2 * MAXPOS + 1
SCALE_A = DQK ** -0.5
KROWS_A = 96
MROW_A = DQK
WIN = 2 * P + MAXPOS
EPS_X = 1e-5
EPS_G = 1e-6
NE = 512
HALF_STEPS = NCHUNK * KB
PIECES = QUAD * KB

NODES = 6
UNITS = NODES * BATCH
SCALE_B = DV ** -0.5
TERMS = ((0, 0), (0, 1), (1, 0), (1, 1), (0, 2), (2, 0))
MROW_B = DV * len(TERMS)
KROWS_B = MROW_B + 3
UNIT_STEPS = 2 * HALF_STEPS
PAIRS = (UNITS - 4) // 2
WP_COLS = 2 * P + 2
WF_COLS = 2 * P + 1

D16 = 16


def edges():
    at, out = 0, []
    for c in range(NODES):
        n = min(c + 1, 5)
        out.append((at + n - 1, at, at + n // 2))
        at += n
    return out


def side(kb, qc):
    r = kb - BPC * qc
    if r in (0, 1):
        return 0, 0, P * (r + 1) + MAXPOS, P - P * r
    if r in (2, 3):
        return 1, P * r - MAXPOS, CHUNK, 0
    if r == BPC:
        return 1, CHUNK - MAXPOS, CHUNK, 0
    if r == -1:
        return 0, 0, MAXPOS, 2 * P
    return (0 if r < 0 else 1), 0, 0, 0


def chain(eng, sem, base):
    n = [0]

    def link(ins):
        n[0] += 1
        ins.then_inc(sem, 1)
        eng.wait_ge(sem, base + n[0])
    return link


def program(nc, x, w_qk, w_v, w_out, b_out, conv, conv_rev, ew, act_w, We, be, Wq, Wk, Wv, Wo, ln_g, ln_b,
            ident, exchange, out):
    def dram(name, shape):
        return nc.dram_tensor(name, shape, F32, kind="Internal").ap()

    xnt = dram("xnt", [BATCH, P, TOK])
    x1d = dram("x1d", [BATCH * NCHUNK, P, BPC, DIM])
    node = dram("node", [UNITS + BATCH, P, TOK])
    ext = dram("ext", [4, HEADS, NE])
    wpd = dram("wpd", [NODES, P, WP_COLS])
    wvd = dram("wvd", [NODES, P, P])
    wfd = dram("wfd", [NODES, P, WF_COLS])
    partd = nc.dram_tensor("partd", [P, 2, 3, TOK], BF16, kind="Internal").ap()
    x_rows = x.rearrange("b (t p) d -> b p t d", p=P)
    out_rows = out.rearrange("b (t p) d -> b p t d", p=P)

    with ExitStack() as ctx:
        def psum(name, n):
            return ctx.enter_context(nc.psum_tensor(name, [P, n], F32))

        psM = [psum(f"ps_max{i}", TOK) for i in range(2)]
        psS = [psum(f"ps_score{i}", CHUNK) for i in range(2)]
        psO = psum("ps_ctx", CHUNK)
        psX = psum("ps_misc", CHUNK)
        sid = ctx.enter_context(nc.sbuf_tensor("ident_sb", [P, P], F32))
        stored = ctx.enter_context(nc.semaphore("node_stored"))

        with nc.sbuf_tensor("tab_scores", [P, 2, HEADS, WIN], F32) as tabS, \
                nc.sbuf_tensor("tab_maxima", [P, 2, HEADS, WIN], F32R) as tabM:
            prelude(nc, psM, psS, psX, sid, exchange, x_rows, conv, conv_rev, ew, act_w, We, be, Wq, Wk, Wv, Wo, ident,
                    xnt, ext, wpd, wvd, wfd, tabS, tabM)
            first_attention(nc, psM, psS, psO, psX, sid, x_rows, w_qk, w_v, w_out, b_out, conv, xnt, x1d, node,
                            tabS, tabM, stored)
        graph(nc, psM, psS, psO, psX, sid, wpd, wvd, wfd, node, partd, stored)
        finish(nc, psM, sid, node, x1d, ln_g, ln_b, out_rows)


def allocators(nc, ctx):
    def sb(name, shape, dt=F32):
        return ctx.enter_context(nc.sbuf_tensor(name, shape, dt))

    def sem(name):
        return ctx.enter_context(nc.semaphore(name))
    return sb, sem


def prelude(nc, psM, psS, psX, sid, exchange, x_rows, conv, conv_rev, ew, act_w, We, be, Wq, Wk, Wv, Wo, ident,
            xnt, ext, wpd, wvd, wfd, tabS, tabM):
    EDGES, EDGE = edges(), We.shape[0]
    with ExitStack() as ctx:
        sb, sem = allocators(nc, ctx)
        xs = sb("xs", [P, BATCH, KB, DIM])
        xn = sb("xn", [P, KB, DIM])
        stats = sb("stats", [P, KB, 6])
        mv = sb("mv", [P, KB, 2])
        sd = sb("sd", [P, KB])
        rs = sb("rs", [P, KB])
        xt = sb("xt", [P, TOK])
        cv = sb("cv", [HEADS, 2, NREL])
        dv_ = sb("ext_plain", [HEADS, 2, NE])
        de = sb("ext_all", [HEADS, 4, NE])
        ewb = sb("ewb", [P, NODES * 3])
        awb = sb("awb", [P, NODES])
        ber = sb("ber", [EDGE, DIM])
        bet = sb("bet", [P, EDGE])
        wein = sb("wein", [P, EDGE, P])
        wnin = sb("wnin", [P, NODES, 4, P])
        wos = sb("wos", [P, NODES, P])
        wet = sb("wet", [P, 3, P])
        bsum = sb("bsum", [P, 2])
        bcol = sb("bcol", [P, 2])
        wps = sb("wps", [P, NODES, WP_COLS])
        wvs = sb("wvs", [P, NODES, P])
        wfs = sb("wfs", [P, NODES, WF_COLS])
        tabf = sb("tabf", [P, 4, HEADS, WIN])
        exch = sb("exch", [P, P])

        x_in = [sem(f"x_in{b}") for b in range(BATCH)]
        w_in, wo_in, small_in, id_in = sem("w_in"), sem("wo_in"), sem("small_in"), sem("id_in")
        ext_ready, ext_out, w_out_s = sem("ext_ready"), sem("ext_out"), sem("w_out_s")
        ve_ready, sd_ready, xn_ready, xt_ready, xt_copied, xt_out = (
            sem("ve_ready"), sem("sd_ready"), sem("xn_ready"), sem("xt_ready"), sem("xt_copied"), sem("xt_out"))
        bias_chain, w_chain, tab_in = sem("bias_chain"), sem("w_chain"), sem("tab_in")
        tab_ready, tab_copied = sem("tab_ready"), [sem("tab_copied0"), sem("tab_copied1")]
        stats_done, aggr_done, rs_done = sem("stats_done"), sem("aggr_done"), sem("rs_done")
        be_ready, be_copied = sem("be_ready"), sem("be_copied")
        wt_ready, wt_copied, wm_ready, wm_copied, wb_ready, wb_copied, wo_ready = (
            sem("wt_ready"), sem("wt_copied"), sem("wm_ready"), sem("wm_copied"), sem("wb_ready"),
            sem("wb_copied"), sem("wo_ready"))

        def table(n):
            return tabS[:, n // HEADS, n % HEADS] if n < 2 * HEADS else tabM[:, n // HEADS - 2, n % HEADS]

        with nc.Block() as block:
            @block.sync
            def _(sp):
                sp.dma_start(sid[:], ident).then_inc(id_in, D16)
                sp.dma_start(exch[:], exchange).then_inc(id_in, D16)
                for b in range(BATCH):
                    sp.dma_start(xs[:, b], x_rows[b]).then_inc(x_in[b], D16)
                    if b:
                        continue
                    sp.dma_start(cv[:, 0], conv_rev).then_inc(small_in, D16)
                    sp.dma_start(cv[:, 1], conv).then_inc(small_in, D16)
                sp.dma_start(ber[:], be).then_inc(small_in, D16)
                sp.dma_start(ewb[:], ew.rearrange("n k -> (n k)").rearrange("(o n) -> o n", o=1)
                             .to_broadcast([P, NODES * 3])).then_inc(small_in, D16)
                sp.dma_start(awb[:], act_w.rearrange("(o n) -> o n", o=1)
                             .to_broadcast([P, NODES])).then_inc(small_in, D16)
                sp.dma_start(wein[:], We.rearrange("e p n -> p e n")).then_inc(w_in, D16)
                for k, w in enumerate((Wq, Wk, Wv, Wo)):
                    sp.dma_start(wnin[:, :, k], w.rearrange("c p n -> p c n")).then_inc(w_in, D16)
                for q in range(2):
                    for i in range(QUAD):
                        rows = Wo[:, (QUAD * q + i) * DV:(QUAD * q + i + 1) * DV, :]
                        at = SLOT * i + DV * q
                        sp.dma_start(wos[at:at + DV],
                                     rows.rearrange("c d n -> d c n")).then_inc(wo_in, D16)
                sp.wait_ge(ext_ready, 1)
                sp.dma_start(ext.rearrange("k h n -> h k n"), de[:]).then_inc(ext_out, D16)
                sp.wait_ge(ext_out, D16)
                for k in range(4):
                    first = NE // 2 - (P, MAXPOS)[k % 2] - (P - 1)
                    sp.dma_start(tabf[:, k], bass.AP(ext.tensor, k * HEADS * NE + first, [[1, P], [NE, HEADS], [1, WIN]])
                                 ).then_inc(tab_in, D16)
                sp.wait_ge(wo_ready, NODES)
                sp.dma_start(wpd.rearrange("c p n -> p c n"), wps[:]).then_inc(w_out_s, D16)
                sp.dma_start(wvd.rearrange("c p n -> p c n"), wvs[:]).then_inc(w_out_s, D16)
                sp.dma_start(wfd.rearrange("c p n -> p c n"), wfs[:]).then_inc(w_out_s, D16)
                sp.wait_ge(w_out_s, 3 * D16)

            @block.tensor
            def _(pe):
                pe.wait_ge(id_in, 2 * D16)
                for b in range(BATCH):
                    pe.wait_ge(xn_ready, b + 1)
                    if b:
                        pe.wait_ge(xt_copied, b)
                    for t in range(KB):
                        ins = pe.transpose(psM[0][:, P * t:P * t + P], xn[:, t], sid[:])
                    ins.then_inc(xt_ready, 1)
                pe.wait_ge(small_in, 5 * D16)
                pe.transpose(psX[:, 0:EDGE], ber[:], sid[0:EDGE, 0:EDGE]).then_inc(be_ready, 1)
                pe.wait_ge(w_in, 5 * D16)
                for c in range(NODES):
                    if c:
                        pe.wait_ge(wt_copied, c)
                    for k in range(3):
                        ins = pe.transpose(psM[1][:, P * k:P * k + P], wein[:, EDGES[c][k]], sid[:])
                    ins.then_inc(wt_ready, 1)
                    pe.wait_ge(wt_copied, c + 1)
                    pe.wait_ge(be_copied, 1)
                    for k in range(3):
                        if c and not k:
                            pe.wait_ge(wm_copied, c)
                        ins = pe.matmul(psM[1][:, CHUNK + P * k:CHUNK + P * k + P], wet[:, k], wnin[:, c, k],
                                        start=True, stop=True)
                    ins.then_inc(wm_ready, 1)
                    if c:
                        pe.wait_ge(wo_ready, c)
                    for k in range(3):
                        ins = pe.matmul(psX[:, 32 + k:33 + k], wnin[:, c, k], bet[:, EDGES[c][k]:EDGES[c][k] + 1],
                                        start=True, stop=True)
                    ins.then_inc(wb_ready, 1)
                    pe.wait_ge(wb_copied, c + 1)
                    pe.matmul(psX[:, 36:37], wnin[:, c, 3], bcol[:, 0:1], start=True, stop=True).then_inc(wb_ready, 1)
                pe.wait_ge(tab_in, 4 * D16)
                for n in range(4 * HEADS):
                    if n >= 2:
                        pe.wait_ge(tab_copied[n % 2], n // 2)
                    pe.matmul(psS[n % 2][:, 0:WIN], exch[:], tabf[:, n // HEADS, n % HEADS], start=True,
                              stop=True).then_inc(tab_ready, 1)

            @block.scalar
            def _(act):
                for b in range(BATCH):
                    act.wait_ge(ve_ready, b + 1)
                    act.activation(sd[:], mv[:, :, 1], ACT.Sqrt).then_inc(sd_ready, 1)
                    act.wait_ge(xt_ready, b + 1)
                    if b:
                        act.wait_ge(xt_out, b * D16)
                    act.activation(xt[:], psM[0][:], ACT.Identity).then_inc(xt_copied, 1)
                    act.wait_ge(xt_copied, b + 1)
                    act.dma_start(xnt[b], xt[:]).then_inc(xt_out, D16)
                for n in range(1, 4 * HEADS, 2):
                    act.wait_ge(tab_ready, n + 1)
                    act.activation(table(n), psS[1][:, 0:WIN], ACT.Identity).then_inc(tab_copied[1], 1)
                act.wait_ge(xt_out, BATCH * D16)

            @block.vector
            def _(dve):
                def extended():
                    dve.wait_ge(small_in, 5 * D16)
                    link = chain(dve, bias_chain, 0)
                    link(nc.vector.memset(dv_[:], 0.0))
                    mid = NE // 2 - MAXPOS
                    for k in range(2):
                        for lo, hi, at in ((0, mid, 0), (mid + NREL, NE, NREL - 1)):
                            link(nc.vector.tensor_scalar(dv_[:, k, lo:hi], dv_[:, k, lo:hi], cv[:, k, at:at + 1], None,
                                                         ALU.add))
                        link(nc.vector.tensor_copy(dv_[:, k, mid:mid + NREL], cv[:, k, :]))
                        for s, at in ((0, NREL - 1), (1, 0)):
                            ins = nc.vector.tensor_scalar(de[:, 2 * k + s], dv_[:, k], cv[:, k, at:at + 1],
                                                          1.0 / SCALE_A, ALU.subtract, ALU.mult)
                    ins.then_inc(ext_ready, 1)

                for b in range(BATCH):
                    if b == 1:
                        extended()
                    dve.wait_ge(x_in[b], D16)
                    for t in range(KB):
                        ins = nc.vector.bn_stats(stats[:, t], xs[:, b, t])
                    ins.then_inc(stats_done, 1)
                    dve.wait_ge(stats_done, b + 1)
                    for t in range(KB):
                        ins = nc.vector.bn_aggr(mv[:, t], stats[:, t])
                    ins.then_inc(aggr_done, 1)
                    dve.wait_ge(aggr_done, b + 1)
                    nc.vector.tensor_scalar(mv[:, :, 1], mv[:, :, 1], EPS_X, None, ALU.add).then_inc(ve_ready, 1)
                    dve.wait_ge(sd_ready, b + 1)
                    nc.vector.reciprocal(rs[:], sd[:]).then_inc(rs_done, 1)
                    dve.wait_ge(rs_done, b + 1)
                    if b:
                        dve.wait_ge(xt_ready, b)
                    for t in range(KB):
                        ins = nc.vector.tensor_scalar(xn[:, t], xs[:, b, t], mv[:, t, 0:1], rs[:, t:t + 1],
                                                      ALU.subtract, ALU.mult)
                    ins.then_inc(xn_ready, 1)

                dve.wait_ge(be_ready, 1)
                nc.vector.tensor_copy(bet[:], psX[:, 0:EDGE]).then_inc(be_copied, 1)
                dve.wait_ge(wo_in, 2 * QUAD * D16)
                for c in range(NODES):
                    s = [ewb[:, 3 * c + k:3 * c + k + 1] for k in range(3)]
                    aw = awb[:, c:c + 1]
                    link = chain(dve, w_chain, 2 * c)
                    dve.wait_ge(wt_ready, c + 1)
                    if c:
                        dve.wait_ge(wm_ready, c)
                    nc.vector.tensor_copy(wet[:], psM[1][:, 0:3 * P].rearrange("p (k n) -> p k n", k=3)).then_inc(wt_copied, 1)
                    dve.wait_ge(wm_ready, c + 1)
                    prod_ps = psM[1][:, CHUNK:CHUNK + 3 * P].rearrange("p (k n) -> p k n", k=3)
                    for k in range(2):
                        nc.vector.tensor_scalar(wps[:, c, P * k:P * k + P], prod_ps[:, k], s[k], None, ALU.mult)
                    nc.vector.tensor_scalar(wvs[:, c], prod_ps[:, 2], s[2], None, ALU.mult).then_inc(wm_copied, 1)
                    dve.wait_ge(wb_ready, 2 * c + 1)
                    for k in range(2):
                        nc.vector.tensor_scalar(wps[:, c, 2 * P + k:2 * P + k + 1], psX[:, 32 + k:33 + k], s[k], None,
                                                ALU.mult)
                    nc.vector.tensor_scalar(bcol[:, 0:1], psX[:, 34:35], s[2], None, ALU.mult).then_inc(wb_copied, 1)
                    nc.vector.tensor_scalar(wfs[:, c, 0:P], wein[:, EDGES[c][0]], s[0], None, ALU.mult)
                    nc.vector.tensor_scalar(wfs[:, c, P:2 * P], wos[:, c], aw, None,
                                            ALU.mult)
                    link(nc.vector.tensor_scalar(bsum[:, 0:1], bet[:, EDGES[c][0]:EDGES[c][0] + 1], s[0], None, ALU.mult))
                    dve.wait_ge(wb_ready, 2 * c + 2)
                    link(nc.vector.tensor_scalar(bsum[:, 1:2], psX[:, 36:37], aw, None, ALU.mult))
                    nc.vector.tensor_tensor(wfs[:, c, 2 * P:2 * P + 1], bsum[:, 0:1], bsum[:, 1:2],
                                            ALU.add).then_inc(wo_ready, 1)
                for n in range(0, 4 * HEADS, 2):
                    dve.wait_ge(tab_ready, n + 1)
                    nc.vector.tensor_copy(table(n), psS[0][:, 0:WIN]).then_inc(tab_copied[0], 1)


def score_ring(last):
    return 6 if last else 2


def score_bank(psS, psM, n, last):
    k = n % score_ring(last)
    return psS[k][:] if k < 2 else psM[k // 2 - 1][:, CHUNK * (k % 2):CHUNK * (k % 2) + CHUNK]


def denominators_turned(nc, dve, c32, den, g, ring, o_copied, den_step, steady):
    copied = known(dve, g + 1)
    dve.wait_ge(steady, 1)
    dve.wait_ge(o_copied, copied)
    nc.vector.transpose(den[:], c32[:, ring]).then_inc(den_step, 1)


def denominators_inverted(nc, dve, den, inv, wide, q, g, cn_done, den_step):
    turned, inverted = known(dve, 3 * g + 1), known(dve, 3 * g + 2)
    if not (isinstance(g, int) and g == 0):
        used = known(dve, g)
        dve.wait_ge(cn_done, used)
    dve.wait_ge(den_step, turned)
    nc.vector.reciprocal(inv[:], den[:].rearrange("p (k r) -> p k r", r=SLOT)[:, :, DV * (1 - q)]).then_inc(den_step, 1)
    dve.wait_ge(den_step, inverted)
    nc.vector.tensor_copy(wide[q][:, :, DV * q:DV * q + DV],
                          inv[:].unsqueeze(2).to_broadcast([P, CHUNK // SLOT, DV])).then_inc(den_step, 1)


def inverses_turned(nc, dve, rec, wide, q, g, rec_ready, den_step, steady):
    spread = known(dve, 3 * g + 3)
    dve.wait_ge(steady, 1)
    dve.wait_ge(den_step, spread)
    nc.vector.transpose(rec[:], wide[q][:].rearrange("p k r -> p (k r)")).then_inc(rec_ready, 1)


def first_attention(nc, psM, psS, psO, psX, sid, x_rows, w_qk, w_v, w_out, b_out, conv, xnt, x1d, node, tabS, tabM,
                    stored):
    with ExitStack() as ctx:
        sb, sem = allocators(nc, ctx)
        khl = [sb(f"khl_{q}", [P, QUAD, TOK], F32R) for q in range(2)]
        qhh = [sb(f"qhh_{q}", [P, QUAD, TOK], F32R) for q in range(2)]
        qlm = [sb(f"qlm_{q}", [KROWS_A, QUAD, TOK], F32R) for q in range(2)]
        khm = sb("khm", [KROWS_A, QUAD, TOK], F32R)
        vs = [sb(f"vs_{q}", [P, KB, QUAD, SLOT]) for q in range(2)]
        pt = sb("pt", [P, 2, QUAD, CHUNK])
        idr = sb("idr", [P, P], F32R)
        xnb = sb("xnb", [P, TOK])
        wqk = sb("wqk", [P, 2 * HEADS * DQK])
        wv = sb("wv_a", [P, P])
        wo = sb("wo_a", [P, P])
        cb = sb("cb", [P, HEADS, NREL])
        cm = sb("cm", [P, HEADS, KB, NCHUNK])
        mx2 = sb("mx2", [P, PIECES, NCHUNK])
        mx3 = sb("mx3", [P, PIECES, NCHUNK])
        mx = sb("mx_a", [P, PIECES])
        mhl = sb("mhl", [PIECES, 2, P], F32R)
        c32 = sb("c32_a", [P, 2, CHUNK])
        den = sb("den_a", [P, CHUNK])
        inv = sb("inv_a", [P, CHUNK // SLOT])
        wide = [sb(f"wide_a{q}", [P, CHUNK // SLOT, SLOT]) for q in range(2)]
        rec = sb("rec_a", [P, CHUNK])
        cn = sb("cn_a", [P, 2, NCHUNK, CHUNK])
        bo = sb("bo", [P, DIM])
        x1 = sb("x1", [P, BPC, DIM])
        stats = sb("stats_a", [P, BPC, 6])
        mv = sb("mv_a", [P, BPC, 2])
        sd = sb("sd_a", [P, BPC])
        rs = sb("rs_a", [P, BPC])
        nt = sb("nt", [P, CHUNK])

        w_in, cb_in = sem("a_w_in"), sem("a_cb_in")
        consts, padded = sem("a_consts"), sem("a_padded")
        xn_in, xr_in = sem("a_xn_in"), sem("a_xr_in")
        pj_ready, pj_high, pj_low, q_twice, k_again = (
            sem("a_pj_ready"), sem("a_pj_high"), sem("a_pj_low"), sem("a_q_twice"), sem("a_k_again"))
        v_ready, v_copied = sem("a_v_ready"), sem("a_v_copied")
        mx_ready, mx_done, mx_biased, mx_final = sem("a_mx_ready"), sem("a_mx_done"), sem("a_mx_biased"), sem("a_mx_final")
        mt_ready, mt_high, mt_copied, mrow = sem("a_mt_ready"), sem("a_mt_high"), sem("a_mt_copied"), sem("a_mrow")
        s_ready, exp_done, pv_done = sem("a_s_ready"), sem("a_exp_done"), sem("a_pv_done")
        cn_alone = sem("a_cn_alone")
        o_copied, den_step, rec_ready, cn_done = sem("a_o_copied"), sem("a_den_step"), sem("a_rec_ready"), sem("a_cn_done")
        fo_ready, fo_copied, x1_ready, x1_out = sem("a_fo_ready"), sem("a_fo_copied"), sem("a_x1_ready"), sem("a_x1_out")
        ve_ready, sd_ready, xh_ready = sem("a_ve_ready"), sem("a_sd_ready"), sem("a_xh_ready")
        stats_done, aggr_done, rs_done = sem("a_stats_done"), sem("a_aggr_done"), sem("a_rs_done")
        ft_ready, ft_copied = sem("a_ft_ready"), sem("a_ft_copied")

        PJ = 8
        PJ_ORDER = [(qk, j, c) for j in range(2) for qk in range(2) for c in range(NCHUNK)]
        TWICE_STEP = {2: 0, 3: 1, 5: 4, 6: 5}
        Q_PJ = [n for n in range(PJ) if not PJ_ORDER[n][0]]
        V_STEP, MT_STEP, FIRST_M, M_STEPS = 4, 15, 4, 11
        FO = {0: 5, 1: 11}
        FT = {0: 8, 1: 14}

        def pieces_at(s):
            first, last = (min(max(0, n), M_STEPS) for n in (s - FIRST_M, s - FIRST_M + 1))
            return range(PIECES * first // M_STEPS, PIECES * last // M_STEPS)

        def pj_bank(n):
            return psM[n % 4 // 2][:, CHUNK * (n % 2):CHUNK * (n % 2) + CHUNK]

        with nc.Block() as block:
            @block.sync
            def _(sp):
                sp.dma_start(xnb[:], xnt[0]).then_inc(xn_in, D16)
                sp.dma_start(wqk[:], w_qk).then_inc(w_in, D16)
                sp.dma_start(wv[:], w_v).then_inc(w_in, D16)
                sp.dma_start(cb[:].rearrange("p h r -> p (h r)"),
                             conv.rearrange("h r -> (h r)").rearrange("(o n) -> o n", o=1)
                             .to_broadcast([P, HEADS * NREL])).then_inc(cb_in, D16)
                sp.dma_start(bo[:], b_out.rearrange("(o n) -> o n", o=1).to_broadcast([P, DIM])).then_inc(w_in, D16)
                for q in range(2):
                    for i in range(QUAD):
                        h = QUAD * q + i
                        sp.dma_start(wo[SLOT * i + DV * q:SLOT * i + DV * q + DV], w_out[h * DV:(h + 1) * DV, :]).then_inc(w_in, D16)

                def maxima(hh, q):
                    sp.wait_ge(mt_copied, hh + 1)
                    for k in range(2):
                        row = qlm[q][MROW_A + k:MROW_A + k + 1, :, :].bitcast(F32)
                        sp.dma_start(row.rearrange("o i (t n) -> o (i t) n", t=KB), mhl[:, k].bitcast(F32)).then_inc(mrow, D16)

                def x1_store(b, c):
                    f = NCHUNK * b + c
                    sp.wait_ge(x1_ready, f + 1)
                    sp.dma_start(x1d[one(f)].rearrange("o p t d -> (o p) t d"), x1[:]).then_inc(x1_out, D16)

                def node_store(b, c):
                    f = NCHUNK * b + c
                    sp.wait_ge(ft_copied, f + 1)
                    sp.dma_start(node[one(b), :, CHUNK * c:CHUNK * c + CHUNK].rearrange("o p n -> (o p) n"),
                                 nt[:]).then_inc(stored, D16)

                def load_rows(b, c):
                    f = NCHUNK * b + c
                    if not (isinstance(f, int) and f == 0):
                        sp.wait_ge(x1_out, f * D16)
                    sp.dma_start(x1[:], x_rows[one(b), :, BPC * c:BPC * c + BPC].rearrange("o p t d -> (o p) t d")
                                 ).then_inc(xr_in, D16)

                def batch(b, first, last):
                    if not first:
                        x1_store(b - 1, 1)
                    if not last:
                        sp.wait_ge(v_ready, 2 * b + 2)
                        sp.dma_start(xnb[:], xnt[one(b + 1)].rearrange("o p n -> (o p) n")).then_inc(xn_in, D16)
                    if not first:
                        node_store(b - 1, 1)
                    load_rows(b, 0)
                    maxima(2 * b + 1, 1)
                    x1_store(b, 0)
                    node_store(b, 0)
                    load_rows(b, 1)
                    if not last:
                        maxima(2 * b + 2, 0)

                sp.wait_ge(padded, 1)
                maxima(0, 0)
                batch(0, True, False)
                with sp.Fori(1, BATCH - 1) as b:
                    batch(b, False, False)
                batch(BATCH - 1, False, True)
                x1_store(BATCH - 1, 1)
                node_store(BATCH - 1, 1)
                sp.wait_ge(x1_out, BATCH * NCHUNK * D16)
                sp.wait_ge(stored, BATCH * NCHUNK * D16)

            @block.tensor
            def _(pe):
                def project(hh, q, n):
                    qk, j, c = PJ_ORDER[n]
                    if q == 0 and n == 0:
                        pe.wait_ge(xn_in, (hh // 2 + 1) * D16)
                    if n >= 4:
                        pe.wait_ge(pj_low, PJ * hh + n - 3)
                    elif n == 0 and not (isinstance(hh, int) and hh == 0):
                        pe.wait_ge(mx_done, PIECES * hh)
                    col = qk * HEADS * DQK + (QUAD * q + 2 * j) * DQK
                    pe.matmul(pj_bank(n), wqk[:, col:col + P], xnb[:, CHUNK * c:CHUNK * c + CHUNK],
                              start=True, stop=True).then_inc(pj_ready, 1)

                def values(hh, q):
                    for kb in range(KB):
                        ins = pe.matmul(psX[:, 64 * kb:64 * kb + 64], xnb[:, P * kb:P * kb + P],
                                        wv[:, 64 * q:64 * q + 64], start=True, stop=True)
                    ins.then_inc(v_ready, 1)

                def maxima(hh, q, p):
                    i, qb = p // KB, p % KB
                    if p < 2:
                        pe.wait_ge(pj_low, PJ * hh + PJ - 2 + 2 * p)
                    if p % (2 * KB) == 0:
                        pe.wait_ge(q_twice, 4 * hh + 2 * (p // (2 * KB) + 1))
                    if not (isinstance(hh, int) and hh == 0 and p < 2):
                        pe.wait_ge(mx_done, PIECES * hh + p - 1)
                    for kc in range(NCHUNK):
                        s, lo, hi, at = side(qb, kc)
                        ins = pe.matmul(psM[p % 2][:, CHUNK * kc:CHUNK * kc + CHUNK], qhh[q][:, i, P * qb:P * qb + P],
                                        khl[q][:, i, CHUNK * kc:CHUNK * kc + CHUNK], start=True, stop=hi == 0)
                        if hi:
                            ins = pe.matmul(psM[p % 2][:, CHUNK * kc + lo:CHUNK * kc + hi], idr[:],
                                            tabM[:, s, QUAD * q + i, at:at + hi - lo], start=False, stop=True)
                    ins.then_inc(mx_ready, 1)

                def turn_maxima(hh):
                    pe.wait_ge(mx_final, hh + 1)
                    pe.transpose(psX[0:PIECES, 0:P], mx[:], sid[:]).then_inc(mt_ready, 1)

                def scores(hh, q, s, i, last):
                    n, ring = QUAD * s + i, score_ring(last)
                    bank = score_bank(psS, psM, n, last)
                    if n == 0:
                        pe.wait_ge(mrow, 2 * (hh + 1) * D16)
                    if n < 2 and not (isinstance(hh, int) and hh == 0):
                        pe.wait_ge(exp_done, QUAD * HALF_STEPS * hh + n - 1)
                    elif n >= ring:
                        pe.wait_ge(exp_done, QUAD * HALF_STEPS * hh + n - ring + 1)
                    elif n == 2:
                        pe.wait_ge(mx_done, PIECES * (hh + 1))
                    kb, qc = s % KB, s // KB
                    if s < KB and i == 0:
                        pe.wait_ge(k_again, KB * hh + kb + 1)
                    sd_, lo, hi, at = side(kb, qc)
                    pe.matmul(bank, khl[q][:, i, P * kb:P * kb + P],
                              qhh[q][:, i, CHUNK * qc:CHUNK * qc + CHUNK], start=True, stop=False)
                    ins = pe.matmul(bank, khm[:, i, P * kb:P * kb + P],
                                    qlm[q][:, i, CHUNK * qc:CHUNK * qc + CHUNK], start=False, stop=hi == 0)
                    if hi:
                        ins = pe.matmul(bank[:, lo:hi], sid[:], tabS[:, sd_, QUAD * q + i, at:at + hi - lo],
                                        start=False, stop=True)
                    ins.then_inc(s_ready, 1)

                def contexts(hh, q, s):
                    kb, g = s % KB, NCHUNK * hh + s // KB
                    if s == 0:
                        pe.wait_ge(v_copied, hh + 1)
                    pe.wait_ge(exp_done, QUAD * (HALF_STEPS * hh + s + 1))
                    if kb == 0 and not (isinstance(g, int) and g == 0):
                        pe.wait_ge(o_copied, g)
                    for i in range(QUAD):
                        ins = pe.matmul(psO[SLOT * i:SLOT * i + SLOT, :], vs[q][:, kb, i], pt[:, s % 2, i],
                                        start=kb == 0, stop=kb == KB - 1)
                    ins.then_inc(pv_done, 1)

                def output(b, c):
                    pe.wait_ge(cn_done, 2 * NCHUNK * b + NCHUNK + c + 1)
                    for t in range(BPC):
                        ins = pe.matmul(psX[:, P * t:P * t + P], cn[:, 1, c, P * t:P * t + P], wo[:],
                                        start=True, stop=True)
                    ins.then_inc(fo_ready, 1)

                def turn_rows(b, c):
                    pe.wait_ge(xh_ready, NCHUNK * b + c + 1)
                    for t in range(BPC):
                        ins = pe.transpose(psX[:, P * t:P * t + P], x1[:, t], sid[:])
                    ins.then_inc(ft_ready, 1)

                def half(hh, b, q, first, last):
                    for s in range(HALF_STEPS):
                        scores(hh, q, s, 0, last)
                        scores(hh, q, s, 1, last)
                        if not last:
                            for p in pieces_at(s)[:2]:
                                maxima(hh + 1, 1 - q, p)
                            if s < PJ // 2:
                                project(hh + 1, 1 - q, 2 * s)
                            if s == V_STEP:
                                pe.wait_ge(mt_copied, hh + 1)
                                values(hh + 1, 1 - q)
                            if s == MT_STEP:
                                if not (first and q == 0):
                                    pe.wait_ge(ft_copied, NCHUNK * b + q)
                                else:
                                    pe.wait_ge(v_copied, hh + 2)
                                turn_maxima(hh + 1)
                        if s == FO[q] and not (first and q == 0):
                            if last:
                                pe.wait_ge(mt_copied, hh + 1)
                            else:
                                pe.wait_ge(v_copied, hh + 2)
                            output(b - 1 + q, 1 - q)
                        if s == FT[q] and not (first and q == 0):
                            pe.wait_ge(fo_copied, NCHUNK * b + q)
                            turn_rows(b - 1 + q, 1 - q)
                        scores(hh, q, s, 2, last)
                        scores(hh, q, s, 3, last)
                        if not last and s < PJ // 2:
                            project(hh + 1, 1 - q, 2 * s + 1)
                        if s:
                            contexts(hh, q, s - 1)
                        elif not (first and q == 0):
                            contexts(hh - 1, 1 - q, HALF_STEPS - 1)
                        if not last:
                            for p in pieces_at(s)[2:]:
                                maxima(hh + 1, 1 - q, p)

                pe.wait_ge(w_in, (3 + 2 * QUAD) * D16)
                pe.wait_ge(consts, 1)
                for n in range(PJ):
                    project(0, 0, n)
                values(0, 0)
                for p in range(PIECES):
                    maxima(0, 0, p)
                pe.wait_ge(v_copied, 1)
                turn_maxima(0)
                pe.wait_ge(padded, 2)
                half(0, 0, 0, True, False)
                half(1, 0, 1, True, False)
                with pe.Fori(1, BATCH - 1) as b:
                    half(2 * b, b, 0, False, False)
                    half(2 * b + 1, b, 1, False, False)
                half(2 * BATCH - 2, BATCH - 1, 0, False, False)
                half(2 * BATCH - 1, BATCH - 1, 1, False, True)
                contexts(2 * BATCH - 1, 1, HALF_STEPS - 1)
                pe.wait_ge(ft_copied, NCHUNK * BATCH - 1)
                output(BATCH - 1, 1)
                pe.wait_ge(fo_copied, NCHUNK * BATCH)
                turn_rows(BATCH - 1, 1)

            @block.scalar
            def _(act):
                def high(hh, q, n):
                    qk, j, c = PJ_ORDER[n]
                    act.wait_ge(pj_ready, PJ * hh + n + 1)
                    for k in range(2):
                        ins = act.activation((qhh, khl)[qk][q][0:DQK, 2 * j + k, CHUNK * c:CHUNK * c + CHUNK],
                                             pj_bank(n)[DQK * k:DQK * k + DQK, :], ACT.Identity)
                    ins.then_inc(pj_high, 1)

                def twice(hh, q, n):
                    j, c = PJ_ORDER[n][1:]
                    heads, cols = slice(2 * j, 2 * j + 2), slice(CHUNK * c, CHUNK * c + CHUNK)
                    act.wait_ge(pj_high, PJ * hh + n + 1)
                    act.activation(qhh[q][DQK:P, heads, cols], qhh[q][0:DQK, heads, cols].bitcast(F32),
                                   ACT.Identity).then_inc(q_twice, 1)

                def values(hh, q):
                    act.wait_ge(v_ready, hh + 1)
                    act.activation(vs[q][:, :, :, DV * q:DV * q + DV], psX[:].rearrange("p (k i d) -> p k i d", k=KB, i=QUAD),
                                   ACT.Identity).then_inc(v_copied, 1)

                def root(b, c):
                    act.wait_ge(ve_ready, NCHUNK * b + c + 1)
                    act.activation(sd[:], mv[:, :, 1], ACT.Sqrt).then_inc(sd_ready, 1)

                def turned(b, c):
                    f = NCHUNK * b + c
                    act.wait_ge(ft_ready, f + 1)
                    if not (isinstance(f, int) and f == 0):
                        act.wait_ge(stored, f * D16)
                    act.activation(nt[:], psX[:], ACT.Identity).then_inc(ft_copied, 1)

                def context_copy(g, ring):
                    act.wait_ge(pv_done, KB * (g + 1))
                    if not (isinstance(g, int) and g < 2):
                        act.wait_ge(cn_done, g - 1)
                    act.activation(c32[:, ring], psO[:], ACT.Identity).then_inc(o_copied, 1)

                def half(hh, b, q, first, last):
                    begin = first and q == 0
                    for s in range(HALF_STEPS):
                        if not (begin and s < 2):
                            act.wait_ge(pv_done, HALF_STEPS * hh + s - 1)
                        at = (0, NREL - 1)[side(s % KB, s // KB)[0]]
                        for i in range(QUAD):
                            n = QUAD * s + i
                            act.wait_ge(s_ready, QUAD * HALF_STEPS * hh + n + 1)
                            act.activation(pt[:, s % 2, i], score_bank(psS, psM, n, last), ACT.Exp, scale=SCALE_A,
                                           bias=cb[:, QUAD * q + i, at:at + 1]
                                           ).then_inc(exp_done, 1)
                            if i == 1:
                                if not last and s == V_STEP:
                                    values(hh + 1, 1 - q)
                                if s == FO[q] + 1 and not begin:
                                    root(b - 1 + q, 1 - q)
                                if s == FT[q] and not begin:
                                    turned(b - 1 + q, 1 - q)
                            if i == 1 and s % KB == 1 and not (begin and s == 1):
                                context_copy(NCHUNK * hh + s // KB - 1, (s // KB + 1) % 2)
                            if i == 0 and not last and s in TWICE_STEP:
                                twice(hh + 1, 1 - q, TWICE_STEP[s])
                            if i >= 2 and not last and s < PJ // 2:
                                high(hh + 1, 1 - q, 2 * s + i - 2)

                act.wait_ge(cb_in, D16)
                act.wait_ge(consts, 1)
                for n in range(PJ):
                    high(0, 0, n)
                for n in Q_PJ:
                    twice(0, 0, n)
                values(0, 0)
                half(0, 0, 0, True, False)
                half(1, 0, 1, True, False)
                with act.Fori(1, BATCH - 1) as b:
                    half(2 * b, b, 0, False, False)
                    half(2 * b + 1, b, 1, False, False)
                half(2 * BATCH - 2, BATCH - 1, 0, False, False)
                half(2 * BATCH - 1, BATCH - 1, 1, False, True)
                context_copy(2 * NCHUNK * BATCH - 1, 1)
                root(BATCH - 1, 1)
                turned(BATCH - 1, 1)

            @block.vector
            def _(dve):
                def low(hh, q, n):
                    qk, j, c = PJ_ORDER[n]
                    cols = slice(CHUNK * c, CHUNK * c + CHUNK)
                    dst = (qlm[q][0:DQK], khl[q][DQK:P])[qk]
                    dve.wait_ge(pj_high, PJ * hh + n + 1)
                    for k in range(2):
                        ins = nc.vector.tensor_tensor(dst[:, 2 * j + k, cols], pj_bank(n)[DQK * k:DQK * k + DQK, :],
                                                      (qhh, khl)[qk][q][0:DQK, 2 * j + k, cols].bitcast(F32),
                                                      ALU.subtract)
                    ins.then_inc(pj_low, 1)

                def maxima(hh, p):
                    dve.wait_ge(mx_ready, PIECES * hh + p + 1)
                    if p == 0 and not (isinstance(hh, int) and hh == 0):
                        dve.wait_ge(mx_final, hh)
                    nc.vector.tensor_reduce(mx2[:, p], psM[p % 2][:].rearrange("p (c n) -> p c n", c=NCHUNK), AX.X,
                                            ALU.max).then_inc(mx_done, 1)

                def maxima_final(hh, q):
                    dve.wait_ge(mx_done, PIECES * (hh + 1))
                    nc.vector.tensor_tensor(mx3[:], mx2[:], cm[:, QUAD * q:QUAD * q + QUAD].rearrange(
                        "p i t c -> p (i t) c"), ALU.add).then_inc(mx_biased, 1)
                    dve.wait_ge(mx_biased, hh + 1)
                    if not (isinstance(hh, int) and hh == 0):
                        dve.wait_ge(mt_ready, hh)
                    nc.vector.tensor_reduce(mx[:], mx3[:], AX.X, ALU.max).then_inc(mx_final, 1)

                def turned_maxima(hh):
                    dve.wait_ge(mt_ready, hh + 1)
                    if not (isinstance(hh, int) and hh == 0):
                        dve.wait_ge(mrow, 2 * hh * D16)
                    nc.vector.tensor_copy(mhl[:, 0], psX[0:PIECES, 0:P]).then_inc(mt_high, 1)
                    dve.wait_ge(mt_high, hh + 1)
                    nc.vector.tensor_tensor(mhl[:, 1], psX[0:PIECES, 0:P], mhl[:, 0].bitcast(F32),
                                            ALU.subtract).then_inc(mt_copied, 1)

                def rows_out(b, c):
                    f = NCHUNK * b + c
                    dve.wait_ge(fo_ready, f + 1)
                    dve.wait_ge(xr_in, (f + 1) * D16)
                    nc.vector.tensor_tensor(x1[:], psX[:].rearrange("p (t d) -> p t d", t=BPC), x1[:],
                                            ALU.add).then_inc(fo_copied, 1)
                    dve.wait_ge(fo_copied, f + 1)
                    nc.vector.tensor_tensor(x1[:], x1[:], bo[:].unsqueeze(1).to_broadcast([P, BPC, DIM]), ALU.add).then_inc(x1_ready, 1)
                    dve.wait_ge(x1_ready, f + 1)
                    for t in range(BPC):
                        ins = nc.vector.bn_stats(stats[:, t], x1[:, t])
                    ins.then_inc(stats_done, 1)
                    dve.wait_ge(consts, 1)
                    dve.wait_ge(stats_done, f + 1)
                    for t in range(BPC):
                        ins = nc.vector.bn_aggr(mv[:, t], stats[:, t])
                    ins.then_inc(aggr_done, 1)
                    dve.wait_ge(aggr_done, f + 1)
                    nc.vector.tensor_scalar(mv[:, :, 1], mv[:, :, 1], EPS_X, None, ALU.add).then_inc(ve_ready, 1)

                def rows_norm(b, c):
                    f = NCHUNK * b + c
                    dve.wait_ge(sd_ready, f + 1)
                    nc.vector.reciprocal(rs[:], sd[:]).then_inc(rs_done, 1)
                    dve.wait_ge(rs_done, f + 1)
                    dve.wait_ge(x1_out, (f + 1) * D16)
                    for t in range(BPC):
                        ins = nc.vector.tensor_scalar(x1[:, t], x1[:, t], mv[:, t, 0:1], rs[:, t:t + 1],
                                                      ALU.subtract, ALU.mult)
                    ins.then_inc(xh_ready, 1)

                def half(hh, b, q, first, last):
                    begin = first and q == 0
                    for s in range(HALF_STEPS):
                        if not last:
                            for p in pieces_at(s)[:2]:
                                maxima(hh + 1, p)
                            if s < PJ // 2:
                                low(hh + 1, 1 - q, 2 * s)
                                low(hh + 1, 1 - q, 2 * s + 1)
                            if s == MT_STEP:
                                turned_maxima(hh + 1)
                        gq, g, ring = (q if s > KB else 1 - q), NCHUNK * hh + s // KB - 1, (s // KB + 1) % 2
                        if s % KB == 1 and not (begin and s == 1):
                            denominators_turned(nc, dve, c32, den, g, ring, o_copied, den_step, consts)
                        if s % KB == 2 and not (begin and s == 2):
                            denominators_inverted(nc, dve, den, inv, wide, gq, g, cn_done, den_step)
                        if s % KB == 3 and not (begin and s == 3):
                            inverses_turned(nc, dve, rec, wide, gq, g, rec_ready, den_step, consts)
                        if s == FO[q] and not begin:
                            rows_out(b - 1 + q, 1 - q)
                        if s == FT[q] - 1 and not begin:
                            rows_norm(b - 1 + q, 1 - q)
                        if not last:
                            for p in pieces_at(s)[2:]:
                                maxima(hh + 1, p)
                            if s == MT_STEP - 1:
                                maxima_final(hh + 1, 1 - q)

                for q in range(2):
                    nc.vector.memset(wide[q][:], 0.0)
                    nc.vector.memset(vs[q][:, :, :, DV * (1 - q):DV * (2 - q)], 1.0)
                nc.vector.tensor_copy(idr[:], sid[:])
                dve.wait_ge(cb_in, D16)
                for t in range(KB):
                    for c in range(NCHUNK):
                        ins = nc.vector.tensor_scalar(cm[:, :, t, c], cb[:, :, (NREL - 1, 0)[side(t, c)[0]]], 1.0 / SCALE_A, None,
                                                      ALU.mult)
                ins.then_inc(consts, 1)
                for n in range(PJ):
                    low(0, 0, n)
                for p in range(PIECES):
                    maxima(0, p)
                maxima_final(0, 0)
                turned_maxima(0)
                half(0, 0, 0, True, False)
                half(1, 0, 1, True, False)
                with dve.Fori(1, BATCH - 1) as b:
                    half(2 * b, b, 0, False, False)
                    half(2 * b + 1, b, 1, False, False)
                half(2 * BATCH - 2, BATCH - 1, 0, False, False)
                half(2 * BATCH - 1, BATCH - 1, 1, False, True)
                g = 2 * NCHUNK * BATCH - 1
                denominators_turned(nc, dve, c32, den, g, 1, o_copied, den_step, consts)
                denominators_inverted(nc, dve, den, inv, wide, 1, g, cn_done, den_step)
                inverses_turned(nc, dve, rec, wide, 1, g, rec_ready, den_step, consts)
                rows_out(BATCH - 1, 1)
                rows_norm(BATCH - 1, 1)

            @block.gpsimd
            def _(pool):
                def normalise(hh, q, c):
                    g = NCHUNK * hh + c
                    pool.wait_ge(rec_ready, g + 1)
                    if not (isinstance(hh, int) and hh < 2):
                        pool.wait_ge(fo_ready, hh - q - NCHUNK + c + 1)
                    if not q:
                        nc.gpsimd.tensor_tensor(cn[:, 0, c], c32[:, c], rec[:], ALU.mult).then_inc(cn_done, 1)
                        return
                    nc.gpsimd.tensor_tensor(cn[:, 1, c], c32[:, c], rec[:], ALU.mult).then_inc(cn_alone, 1)
                    pool.wait_ge(cn_alone, hh + c)
                    nc.gpsimd.tensor_tensor(cn[:, 1, c], cn[:, 1, c], cn[:, 0, c], ALU.add).then_inc(cn_done, 1)

                def again(hh, q, kb):
                    start = isinstance(hh, int) and hh == 0
                    if start and kb == 0:
                        pool.wait_ge(pj_high, PJ)
                    if not start:
                        used = known(pool, QUAD * (HALF_STEPS * (hh - 1) + KB + kb + 1))
                        pool.wait_ge(consts, 1)
                        pool.wait_ge(s_ready, used)
                    cols = slice(P * kb, P * kb + P)
                    nc.gpsimd.tensor_scalar(khm[0:DQK, :, cols], khl[q][0:DQK, :, cols].bitcast(F32), 0.0, None, ALU.add
                                            ).then_inc(k_again, 1)

                def half(hh, q, first, last):
                    if not (first and q == 0):
                        normalise(hh - 1, 1 - q, 1)
                    if not last:
                        for kb in range(2):
                            again(hh + 1, 1 - q, kb)
                    normalise(hh, q, 0)
                    if not last:
                        for kb in range(2, KB):
                            again(hh + 1, 1 - q, kb)

                for q in range(2):
                    nc.gpsimd.memset(qlm[q][DQK:KROWS_A].bitcast(F32), 0.0)
                nc.gpsimd.memset(khm[DQK:KROWS_A].bitcast(F32), 0.0).then_inc(padded, 1)
                pool.wait_ge(padded, 1)
                nc.gpsimd.memset(khm[MROW_A:MROW_A + 2].bitcast(F32), -1.0).then_inc(padded, 1)
                for kb in range(KB):
                    again(0, 0, kb)
                half(0, 0, True, False)
                half(1, 1, True, False)
                with pool.Fori(1, BATCH - 1) as b:
                    half(2 * b, 0, False, False)
                    half(2 * b + 1, 1, False, False)
                half(2 * BATCH - 2, 0, False, False)
                half(2 * BATCH - 1, 1, False, True)
                normalise(2 * BATCH - 1, 1, 1)


def known(eng, value):
    return value if isinstance(value, int) else eng.snap(eng.to_reg(value))


def one(i):
    return slice(i, i + 1) if isinstance(i, int) else bass.ds(i, 1)


def graph(nc, psM, psS, psO, psX, sid, wpd, wvd, wfd, node, partd, stored):
    with ExitStack() as ctx:
        sb, sem = allocators(nc, ctx)
        qs = [sb(f"qs{i}", [KROWS_B, HEADS, TOK], BF16) for i in range(2)]
        ks = [sb(f"ks{i}", [P, HEADS, TOK], BF16) for i in range(2)]
        vs = [sb(f"vs{i}", [P, KB, HEADS, SLOT]) for i in range(2)]
        pt = sb("pt_b", [P, 2, QUAD, CHUNK])
        part = sb("part", [P, 2, 3, TOK], BF16)
        full = sb("full", [P, 2, TOK])
        rest = sb("rest", [P, CHUNK])
        xq, xk, xv, xf = sb("xq", [P, TOK]), sb("xk", [P, TOK]), sb("xv", [P, TOK]), sb("xf", [P, TOK])
        wp, wv, wf = sb("wp", [P, WP_COLS]), sb("wv_b", [P, P]), sb("wf", [P, WF_COLS])
        mx = sb("mx_b", [P, 2 * PIECES])
        m32, mrest = sb("m32_b", [PIECES, P]), sb("mrest", [PIECES, P])
        mpart = sb("mpart", [PIECES, 3, P], BF16)
        c32, rec = sb("c32_b", [P, 2, CHUNK]), sb("rec_b", [P, CHUNK])
        den, inv = sb("den_b", [P, CHUNK]), sb("inv_b", [P, CHUNK // SLOT])
        wide = [sb(f"wide_b{q}", [P, CHUNK // SLOT, SLOT]) for q in range(2)]
        cn = sb("cn_b", [P, 2, NCHUNK, CHUNK])
        nt = sb("nt_b", [P, NCHUNK, CHUNK])

        ones = sem("b_ones")
        minus = sem("b_minus")
        p_in, v_in, f_in = sem("b_p_in"), sem("b_v_in"), sem("b_f_in")
        pj_ready, pj_copied, split_done, rest_done = (
            sem("b_pj_ready"), sem("b_pj_copied"), sem("b_split_done"), sem("b_rest_done"))
        spilled = sem("b_spilled")
        stacked = [sem("b_stacked0"), sem("b_stacked1")]
        v_ready, v_copied = sem("b_v_ready"), sem("b_v_copied")
        mx_ready, mx_done = sem("b_mx_ready"), sem("b_mx_done")
        mt_ready, mt_copied, mp_step, mp_done = sem("b_mt_ready"), sem("b_mt_copied"), sem("b_mp_step"), sem("b_mp_done")
        mrow = [sem("b_mrow0"), sem("b_mrow1")]
        s_ready, exp_done, pv_done = sem("b_s_ready"), sem("b_exp_done"), sem("b_pv_done")
        cn_alone = sem("b_cn_alone")
        o_copied, den_step, rec_ready, cn_done = sem("b_o_copied"), sem("b_den_step"), sem("b_rec_ready"), sem("b_cn_done")
        fin_ready, fin_copied = sem("b_fin_ready"), sem("b_fin_copied")

        PJ = 2 * NCHUNK
        NS = QUAD * UNIT_STEPS
        NM = 2 * PIECES
        NG = 2 * NCHUNK
        STACK = 2 * len(TERMS) * D16
        PER_STEP = NM // UNIT_STEPS
        PJ_STEP = {10: 0, 12: 1, 14: 2, 16: 3}
        V_STEP = {6: 0, 8: 1}
        MT1_STEP, FIN1_STEP, MT0_STEP, FIN0_STEP = 1, 5, 18, 29
        AHEAD = PIECES + 4
        MT_FIRST = (23, 13)
        GROUP_STEP = {KB * g + 1: g for g in range(NG)}

        def is_first(u):
            return isinstance(u, int) and u == 0

        def pieces_at(u, s, look):
            if is_first(u):
                return ([(0, p) for p in range(AHEAD, NM)] + [(1, p) for p in range(NM)])[3 * s:3 * s + 3]
            return [(u + 1, p) for p in range(PER_STEP * s, PER_STEP * (s + 1))] if look >= 1 else []

        def is_mt(u, s, q):
            return s == (MT_FIRST[q] if is_first(u) else (MT0_STEP, MT1_STEP)[q])

        def split(eng, vec, w, n):
            qk, c = n // NCHUNK, n % NCHUNK
            cols = slice(CHUNK * c, CHUNK * c + CHUNK)
            eng.wait_ge(pj_copied, PJ * w + n + 1)
            if not (is_first(w) and n == 0):
                eng.wait_ge(split_done, PJ * w + n)
            vec.tensor_tensor(part[:, qk, 1, cols], full[:, qk, cols], part[:, qk, 0, cols], ALU.subtract)
            vec.tensor_tensor(rest[:], full[:, qk, cols], part[:, qk, 0, cols], ALU.subtract).then_inc(rest_done, 1)
            eng.wait_ge(rest_done, PJ * w + n + 1)
            vec.tensor_tensor(part[:, qk, 2, cols], rest[:], part[:, qk, 1, cols], ALU.subtract).then_inc(split_done, 1)

        with nc.Block() as block:
            @block.sync
            def _(sp):
                def row(t, i):
                    return t[one(i)].rearrange("o p n -> (o p) n")

                def at(value):
                    return known(sp, value)

                def load_projection(w):
                    used, there = at(PJ * w), at(NCHUNK * D16 * (w + 1))
                    c, query_at = at(w // BATCH), at(w)
                    key_at = at(w % BATCH + w // (5 * BATCH) * BATCH)
                    if not is_first(w):
                        sp.wait_ge(pj_copied, used)
                    sp.wait_ge(stored, there)
                    sp.dma_start(wp[:], row(wpd, c)).then_inc(p_in, D16)
                    sp.dma_start(xq[:], row(node, query_at)).then_inc(p_in, D16)
                    sp.dma_start(xk[:], row(node, key_at)).then_inc(p_in, D16)

                def load_values(w):
                    used, there = at(2 * w), at(NCHUNK * D16 * (w + 1))
                    c, value_at = at(w // BATCH), at((w // BATCH + 1) // 2 * BATCH + w % BATCH)
                    if not is_first(w):
                        sp.wait_ge(v_ready, used)
                    sp.wait_ge(stored, there)
                    sp.dma_start(wv[:], row(wvd, c)).then_inc(v_in, D16)
                    sp.dma_start(xv[:], row(node, value_at)).then_inc(v_in, D16)

                def load_residual(u):
                    used, c, query_at = at(NCHUNK * u), at(u // BATCH), at(u)
                    if not is_first(u):
                        sp.wait_ge(fin_copied, used)
                    sp.dma_start(wf[:], row(wfd, c)).then_inc(f_in, D16)
                    sp.dma_start(xf[:], row(node, query_at)).then_inc(f_in, D16)

                def spill(w):
                    sp.wait_ge(split_done, PJ * (w + 1))
                    sp.dma_start(partd, part[:]).then_inc(spilled, D16)

                def stack(w, par, q):
                    there = at(D16 * (w + 1))
                    free = at(NS * (w - 2) + NS // 2 * (q + 1))
                    if not (isinstance(w, int) and w < 2):
                        sp.wait_ge(s_ready, free)
                    sp.wait_ge(spilled, there)
                    for t, (a, b) in enumerate(TERMS):
                        for qk, dst, k in ((0, qs, a), (1, ks, b)):
                            src = partd[:, qk, k].rearrange("(h d) t -> d h t", d=DV)
                            sp.dma_start(dst[par][DV * t:DV * t + DV, QUAD * q:QUAD * q + QUAD, :],
                                         src[:, QUAD * q:QUAD * q + QUAD]).then_inc(stacked[q], D16)

                def maxima_rows(w, par, q):
                    sp.wait_ge(mp_done, 2 * w + q + 1)
                    for k in range(3):
                        dst = qs[par][MROW_B + k:MROW_B + k + 1, QUAD * q:QUAD * q + QUAD, :]
                        sp.dma_start(dst.rearrange("o i (t n) -> o (i t) n", t=KB), mpart[:, k]).then_inc(mrow[q], D16)

                def store(u, c):
                    ready, before = at(NCHUNK * u + c + 1), at(D16 * (NCHUNK * (u + BATCH) + c))
                    entry = at(u + BATCH)
                    sp.wait_ge(fin_copied, ready)
                    if not (is_first(u) and c == 0):
                        sp.wait_ge(stored, before)
                    sp.dma_start(node[one(entry), :, CHUNK * c:CHUNK * c + CHUNK].rearrange("o p n -> (o p) n"),
                                 nt[:, c]).then_inc(stored, D16)

                def unit(u, par, look):
                    if look >= 1:
                        stack(u + 1, 1 - par, 1)
                    if look >= 2:
                        load_projection(u + 2)
                    if look >= 1:
                        load_values(u + 1)
                    maxima_rows(u, par, 1)
                    if not is_first(u):
                        store(u - 1, 1)
                    load_residual(u)
                    if look >= 2:
                        spill(u + 2)
                        stack(u + 2, par, 0)
                    if look >= 1:
                        maxima_rows(u + 1, 1 - par, 0)
                    store(u, 0)

                load_projection(0)
                load_values(0)
                load_projection(1)
                spill(0)
                stack(0, 0, 0)
                stack(0, 0, 1)
                spill(1)
                maxima_rows(0, 0, 0)
                stack(1, 1, 0)
                unit(0, 0, 2)
                with sp.Fori(0, PAIRS) as i:
                    unit(2 * i + 1, 1, 2)
                    unit(2 * i + 2, 0, 2)
                unit(UNITS - 3, 1, 2)
                unit(UNITS - 2, 0, 1)
                unit(UNITS - 1, 1, 0)
                store(UNITS - 1, 1)
                sp.wait_ge(stored, (UNITS + BATCH) * NCHUNK * D16)

            @block.tensor
            def _(pe):
                def project(w, n):
                    qk, c = n // NCHUNK, n % NCHUNK
                    if n == 0:
                        pe.wait_ge(p_in, 3 * D16 * (w + 1))
                    pe.matmul(psX[:], wp[:, P * qk:P * qk + P], (xq, xk)[qk][:, CHUNK * c:CHUNK * c + CHUNK],
                              start=True, stop=True).then_inc(pj_ready, 1)

                def values(w, n):
                    if n == 0:
                        pe.wait_ge(v_in, 2 * D16 * (w + 1))
                    for t in range(BPC):
                        kb = BPC * n + t
                        ins = pe.matmul(psX[:, P * t:P * t + P], xv[:, P * kb:P * kb + P], wv[:],
                                        start=True, stop=True)
                    ins.then_inc(v_ready, 1)

                def maxima(w, par, p):
                    h, qb = p // KB, p % KB
                    if p % PIECES == 0:
                        pe.wait_ge(stacked[p // PIECES], STACK * (w + 1))
                    if not (is_first(w) and p < 2):
                        pe.wait_ge(mx_done, NM * w + p - 1)
                    for kc in range(NCHUNK):
                        ins = pe.matmul(psM[p % 2][:, CHUNK * kc:CHUNK * kc + CHUNK],
                                        qs[par][0:MROW_B, h, P * qb:P * qb + P],
                                        ks[par][0:MROW_B, h, CHUNK * kc:CHUNK * kc + CHUNK], start=True, stop=True)
                    ins.then_inc(mx_ready, 1)

                def turn_maxima(w, q):
                    pe.wait_ge(mx_done, NM * w + PIECES * (q + 1))
                    pe.transpose(psX[0:PIECES, 0:P], mx[:, PIECES * q:PIECES * q + PIECES], sid[:]).then_inc(mt_ready, 1)

                def scores(u, par, s, i, last):
                    n, ring = QUAD * s + i, score_ring(last)
                    if n % (NS // 2) == 0:
                        pe.wait_ge(mrow[s // HALF_STEPS], 3 * D16 * (u + 1))
                    if n < 2 and not is_first(u):
                        pe.wait_ge(exp_done, NS * u + n - 1)
                    elif n >= ring:
                        pe.wait_ge(exp_done, NS * u + n - ring + 1)
                    elif n == 2:
                        pe.wait_ge(mx_done, NM * (u + 1))
                    h, qc, kb = QUAD * (s // HALF_STEPS) + i, s // KB % NCHUNK, s % KB
                    pe.matmul(score_bank(psS, psM, n, last), ks[par][0:KROWS_B, h, P * kb:P * kb + P],
                              qs[par][0:KROWS_B, h, CHUNK * qc:CHUNK * qc + CHUNK],
                              start=True, stop=True).then_inc(s_ready, 1)

                def contexts(u, par, s):
                    kb, g = s % KB, s // KB
                    if s == 0:
                        pe.wait_ge(v_copied, 2 * (u + 1))
                    pe.wait_ge(exp_done, NS * u + QUAD * (s + 1))
                    if kb == 0 and not (is_first(u) and g == 0):
                        pe.wait_ge(o_copied, NG * u + g)
                    for i in range(QUAD):
                        ins = pe.matmul(psO[SLOT * i:SLOT * i + SLOT, :], vs[par][:, kb, QUAD * (s // HALF_STEPS) + i],
                                        pt[:, s % 2, i], start=kb == 0, stop=kb == KB - 1)
                    ins.then_inc(pv_done, 1)

                def output(u, c):
                    pe.wait_ge(f_in, 2 * D16 * (u + 1))
                    pe.wait_ge(cn_done, NG * u + NCHUNK + c + 1)
                    pe.matmul(psX[:], wf[:, 0:P], xf[:, CHUNK * c:CHUNK * c + CHUNK], start=True, stop=False)
                    pe.matmul(psX[:], wf[:, P:2 * P], cn[:, 1, c], start=False, stop=True).then_inc(fin_ready, 1)

                def unit(u, par, look):
                    for s in range(UNIT_STEPS):
                        scores(u, par, s, 0, look == 0)
                        scores(u, par, s, 1, look == 0)
                        for w, p in pieces_at(u, s, look)[:2]:
                            maxima(w, 0 if is_first(w) else 1 - par, p)
                        if is_mt(u, s, 1):
                            if is_first(u):
                                pe.wait_ge(pj_copied, PJ * 2 + 2)
                            else:
                                pe.wait_ge(fin_copied, NCHUNK * u - 1)
                            turn_maxima(u, 1)
                        if s == FIN1_STEP and not is_first(u):
                            pe.wait_ge(mt_copied, 2 * (u + 1))
                            output(u - 1, 1)
                        if s in V_STEP and look >= 1:
                            if V_STEP[s]:
                                pe.wait_ge(v_copied, 2 * (u + 1) + 1)
                            elif is_first(u):
                                pe.wait_ge(mt_copied, 1)
                            else:
                                pe.wait_ge(fin_copied, NCHUNK * u)
                            values(u + 1, V_STEP[s])
                        if s in PJ_STEP and look >= 2:
                            if PJ_STEP[s]:
                                pe.wait_ge(pj_copied, PJ * (u + 2) + PJ_STEP[s])
                                if is_first(u) and PJ_STEP[s] == 2:
                                    pe.wait_ge(mt_copied, 2)
                            else:
                                pe.wait_ge(v_copied, 2 * (u + 2))
                            project(u + 2, PJ_STEP[s])
                        if is_mt(u, s, 0) and look >= 1:
                            if look >= 2:
                                pe.wait_ge(pj_copied, PJ * (u + 3))
                            else:
                                pe.wait_ge(v_copied, 2 * (u + 2))
                            turn_maxima(u + 1, 0)
                        if s == FIN0_STEP:
                            if look >= 1:
                                pe.wait_ge(mt_copied, 2 * (u + 1) + 1)
                            else:
                                pe.wait_ge(fin_copied, NCHUNK * u)
                            output(u, 0)
                        scores(u, par, s, 2, look == 0)
                        scores(u, par, s, 3, look == 0)
                        if s:
                            contexts(u, par, s - 1)
                        elif not is_first(u):
                            contexts(u - 1, 1 - par, UNIT_STEPS - 1)
                        for w, p in pieces_at(u, s, look)[2:]:
                            maxima(w, 0 if is_first(w) else 1 - par, p)

                for n in range(PJ):
                    if n:
                        pe.wait_ge(pj_copied, n)
                    project(0, n)
                for n in range(2):
                    if n:
                        pe.wait_ge(v_copied, n)
                    else:
                        pe.wait_ge(pj_copied, PJ)
                    values(0, n)
                for p in range(AHEAD):
                    maxima(0, 0, p)
                    n = p // 4
                    if p % 4 == 3 and n < PJ:
                        if n:
                            pe.wait_ge(pj_copied, PJ + n)
                        else:
                            pe.wait_ge(v_copied, 2)
                        project(1, n)
                    if p == PIECES + 1:
                        pe.wait_ge(pj_copied, 2 * PJ)
                        turn_maxima(0, 0)
                pe.wait_ge(minus, 1)
                unit(0, 0, 2)
                with pe.Fori(0, PAIRS) as i:
                    unit(2 * i + 1, 1, 2)
                    unit(2 * i + 2, 0, 2)
                unit(UNITS - 3, 1, 2)
                unit(UNITS - 2, 0, 1)
                unit(UNITS - 1, 1, 0)
                contexts(UNITS - 1, 1, UNIT_STEPS - 1)
                pe.wait_ge(fin_copied, NCHUNK * UNITS - 1)
                output(UNITS - 1, 1)

            @block.scalar
            def _(act):
                def project(w, n):
                    qk, c = n // NCHUNK, n % NCHUNK
                    cols = slice(CHUNK * c, CHUNK * c + CHUNK)
                    act.wait_ge(pj_ready, PJ * w + n + 1)
                    if n == 0 and not is_first(w):
                        act.wait_ge(stacked[1], STACK * w)
                    act.activation(full[:, qk, cols], psX[:], ACT.Identity, bias=wp[:, 2 * P + qk:2 * P + qk + 1])

                def high(n):
                    qk, c = n // NCHUNK, n % NCHUNK
                    cols = slice(CHUNK * c, CHUNK * c + CHUNK)
                    act.activation(part[:, qk, 0, cols], psX[:], ACT.Identity,
                                   bias=wp[:, 2 * P + qk:2 * P + qk + 1]).then_inc(pj_copied, 1)

                def values(w, par, n):
                    act.wait_ge(v_ready, 2 * w + n + 1)
                    for q in range(2):
                        heads = slice(QUAD * q, QUAD * q + QUAD)
                        ins = act.activation(vs[par][:, BPC * n:BPC * n + BPC, heads, DV * q:DV * q + DV],
                                             psX[:].rearrange("p (k h d) -> p k h d", k=BPC, h=HEADS)[:, :, heads],
                                             ACT.Identity)
                    ins.then_inc(v_copied, 1)

                def turned_maxima(w, q):
                    act.wait_ge(mt_ready, 2 * w + q + 1)
                    if q:
                        act.wait_ge(mrow[0], 3 * D16 * (w + 1))
                    elif not is_first(w):
                        act.wait_ge(mrow[1], 3 * D16 * w)
                    act.activation(m32[:], psX[0:PIECES, 0:P], ACT.Identity)
                    act.activation(mpart[:, 0], psX[0:PIECES, 0:P], ACT.Identity).then_inc(mt_copied, 1)

                def output(u, c):
                    act.wait_ge(fin_ready, NCHUNK * u + c + 1)
                    if not is_first(u):
                        act.wait_ge(stored, D16 * (NCHUNK * (u - 1 + BATCH) + c + 1))
                    act.activation(nt[:, c], psX[:], ACT.Identity, bias=wf[:, 2 * P:2 * P + 1]).then_inc(fin_copied, 1)

                def context_copy(u, g):
                    act.wait_ge(pv_done, UNIT_STEPS * u + KB * (g + 1))
                    if not (is_first(u) and g < 2):
                        act.wait_ge(cn_done, NG * u + g - 1)
                    act.activation(c32[:, g % 2], psO[:], ACT.Identity).then_inc(o_copied, 1)

                def unit(u, par, look):
                    for s in range(UNIT_STEPS):
                        if not (is_first(u) and s < 2):
                            act.wait_ge(pv_done, UNIT_STEPS * u + s - 1)
                        for i in range(QUAD):
                            n = QUAD * s + i
                            act.wait_ge(s_ready, NS * u + n + 1)
                            act.activation(pt[:, s % 2, i], score_bank(psS, psM, n, look == 0), ACT.Exp, scale=SCALE_B
                                           ).then_inc(exp_done, 1)
                            if i == 1 and s in GROUP_STEP and not (is_first(u) and s == 1):
                                if s == 1:
                                    context_copy(u - 1, NG - 1)
                                else:
                                    context_copy(u, GROUP_STEP[s] - 1)
                            if i == QUAD - 1:
                                if is_mt(u, s, 1):
                                    turned_maxima(u, 1)
                                if is_mt(u, s, 0) and look >= 1:
                                    turned_maxima(u + 1, 0)
                                if s == FIN1_STEP and not is_first(u):
                                    output(u - 1, 1)
                                if s in V_STEP and look >= 1:
                                    values(u + 1, 1 - par, V_STEP[s])
                                if s in PJ_STEP and look >= 2:
                                    project(u + 2, PJ_STEP[s])
                                if s == FIN0_STEP:
                                    output(u, 0)
                            if i == 1 and s - 1 in PJ_STEP and look >= 2:
                                high(PJ_STEP[s - 1])

                for n in range(PJ):
                    project(0, n)
                    high(n)
                act.wait_ge(ones, 1)
                for n in range(2):
                    values(0, 0, n)
                for n in range(PJ):
                    project(1, n)
                    high(n)
                turned_maxima(0, 0)
                unit(0, 0, 2)
                with act.Fori(0, PAIRS) as i:
                    unit(2 * i + 1, 1, 2)
                    unit(2 * i + 2, 0, 2)
                unit(UNITS - 3, 1, 2)
                unit(UNITS - 2, 0, 1)
                unit(UNITS - 1, 1, 0)
                context_copy(UNITS - 1, NG - 1)
                output(UNITS - 1, 1)

            @block.vector
            def _(dve):
                def maxima(w, p):
                    dve.wait_ge(mx_ready, NM * w + p + 1)
                    if p % PIECES == 0 and not is_first(w):
                        dve.wait_ge(mt_ready, 2 * w - 1 + p // PIECES)
                    nc.vector.tensor_reduce(mx[:, p:p + 1], psM[p % 2][:], AX.X, ALU.max).then_inc(mx_done, 1)

                def unit(u, par, look):
                    for s in range(UNIT_STEPS):
                        for w, p in pieces_at(u, s, look)[:2]:
                            maxima(w, p)
                        n = s // KB - 1
                        g = NG * u + n
                        if s % KB == 1 and not (is_first(u) and s == 1):
                            denominators_turned(nc, dve, c32, den, g, n % 2, o_copied, den_step, ones)
                        if s % KB == 2 and not (is_first(u) and s == 2):
                            denominators_inverted(nc, dve, den, inv, wide, n // 2 % 2, g, cn_done, den_step)
                        if s % KB == 3 and not (is_first(u) and s == 3):
                            inverses_turned(nc, dve, rec, wide, n // 2 % 2, g, rec_ready, den_step, ones)
                        for w, p in pieces_at(u, s, look)[2:]:
                            maxima(w, p)

                for i in range(2):
                    nc.vector.memset(wide[i][:], 0.0)
                    for q in range(2):
                        ins = nc.vector.memset(vs[i][:, :, QUAD * q:QUAD * q + QUAD, DV * (1 - q):DV * (2 - q)], 1.0)
                ins.then_inc(ones, 1)
                for n in range(PJ):
                    split(dve, nc.vector, 0, n)
                for i in range(2):
                    ins = nc.vector.memset(ks[i][MROW_B:P], -1.0)
                ins.then_inc(minus, 1)
                for p in range(AHEAD):
                    maxima(0, p)
                unit(0, 0, 2)
                with dve.Fori(0, PAIRS) as i:
                    unit(2 * i + 1, 1, 2)
                    unit(2 * i + 2, 0, 2)
                unit(UNITS - 3, 1, 2)
                unit(UNITS - 2, 0, 1)
                unit(UNITS - 1, 1, 0)
                g = NG * UNITS - 1
                denominators_turned(nc, dve, c32, den, g, 1, o_copied, den_step, ones)
                denominators_inverted(nc, dve, den, inv, wide, 1, g, cn_done, den_step)
                inverses_turned(nc, dve, rec, wide, 1, g, rec_ready, den_step, ones)

            @block.gpsimd
            def _(pool):
                def split_maxima(w, q):
                    pool.wait_ge(mt_copied, 2 * w + q + 1)
                    nc.gpsimd.tensor_tensor(mpart[:, 1], m32[:], mpart[:, 0], ALU.subtract)
                    nc.gpsimd.tensor_tensor(mrest[:], m32[:], mpart[:, 0], ALU.subtract).then_inc(mp_step, 1)
                    pool.wait_ge(mp_step, 2 * w + q + 1)
                    nc.gpsimd.tensor_tensor(mpart[:, 2], mrest[:], mpart[:, 1], ALU.subtract).then_inc(mp_done, 1)

                def normalise(u, g):
                    pool.wait_ge(rec_ready, NG * u + g + 1)
                    if not is_first(u):
                        pool.wait_ge(fin_ready, NCHUNK * (u - 1) + g % 2 + 1)
                    c = g % 2
                    if g < 2:
                        nc.gpsimd.tensor_tensor(cn[:, 0, c], c32[:, c], rec[:], ALU.mult).then_inc(cn_done, 1)
                        return
                    nc.gpsimd.tensor_tensor(cn[:, 1, c], c32[:, c], rec[:], ALU.mult).then_inc(cn_alone, 1)
                    pool.wait_ge(cn_alone, NCHUNK * u + c + 1)
                    nc.gpsimd.tensor_tensor(cn[:, 1, c], cn[:, 1, c], cn[:, 0, c], ALU.add).then_inc(cn_done, 1)

                def unit(u, look):
                    normalise(u - 1, NG - 1)
                    split_maxima(u, 1)
                    if look >= 2:
                        split(pool, nc.gpsimd, u + 2, 0)
                    normalise(u, 0)
                    if look >= 2:
                        for n in range(1, PJ):
                            split(pool, nc.gpsimd, u + 2, n)
                    normalise(u, 1)
                    if look >= 1:
                        split_maxima(u + 1, 0)
                    normalise(u, 2)

                for n in range(PJ):
                    split(pool, nc.gpsimd, 1, n)
                split_maxima(0, 0)
                split(pool, nc.gpsimd, 2, 0)
                normalise(0, 0)
                split(pool, nc.gpsimd, 2, 1)
                split_maxima(0, 1)
                split(pool, nc.gpsimd, 2, 2)
                split(pool, nc.gpsimd, 2, 3)
                normalise(0, 1)
                split_maxima(1, 0)
                normalise(0, 2)
                with pool.Fori(0, PAIRS) as i:
                    unit(2 * i + 1, 2)
                    unit(2 * i + 2, 2)
                unit(UNITS - 3, 2)
                unit(UNITS - 2, 1)
                unit(UNITS - 1, 0)
                normalise(UNITS - 1, NG - 1)


def finish(nc, psM, sid, node, x1d, ln_g, ln_b, out_rows):
    with ExitStack() as ctx:
        sb, sem = allocators(nc, ctx)
        nin = sb("nin", [P, 2, TOK])
        x1 = sb("x1_c", [P, BATCH, KB, DIM])
        gb = sb("gb", [P, 2, DIM])
        yn = sb("yn", [P, 2, KB, DIM])
        yb = sb("yb", [P, BATCH, KB, DIM])
        yo = sb("yo", [P, 2, KB, DIM])
        stats = sb("stats_c", [P, KB, 6])
        mv = sb("mv_c", [P, KB, 2])
        sd, rs = sb("sd_c", [P, KB]), sb("rs_c", [P, KB])
        n_in, x_in = [sem("c_n_in0"), sem("c_n_in1")], [sem(f"c_x_in{b}") for b in range(BATCH)]
        based, gained = sem("c_based"), sem("c_gained")
        gb_in, turned, ve_ready, sd_ready, scaled = (
            sem("c_gb_in"), sem("c_turned"), sem("c_ve_ready"), sem("c_sd_ready"), sem("c_scaled"))
        step, y_ready, y_out = sem("c_step"), sem("c_y_ready"), sem("c_y_out")
        LINKS = 3

        with nc.Block() as block:
            @block.sync
            def _(sp):
                for k, w in enumerate((ln_g, ln_b)):
                    sp.dma_start(gb[:, k], w.rearrange("(o n) -> o n", o=1).to_broadcast([P, DIM])).then_inc(gb_in, D16)
                for b in range(BATCH):
                    if b >= 2:
                        sp.wait_ge(turned, b - 1)
                    sp.dma_start(nin[:, b % 2], node[UNITS + b]).then_inc(n_in[b % 2], D16)
                    for c in range(NCHUNK):
                        sp.dma_start(x1[:, b, BPC * c:BPC * c + BPC], x1d[NCHUNK * b + c]).then_inc(x_in[b], D16)
                for b in range(BATCH):
                    sp.wait_ge(y_ready, b + 1)
                    sp.dma_start(out_rows[b], yo[:, b % 2]).then_inc(y_out, D16)
                    sp.wait_ge(y_out, (b + 1) * D16)

            @block.tensor
            def _(pe):
                for b in range(BATCH):
                    pe.wait_ge(n_in[b % 2], (b // 2 + 1) * D16)
                    if b >= 2:
                        pe.wait_ge(scaled, b - 1)
                    for t in range(KB):
                        ins = pe.transpose(psM[b % 2][:, P * t:P * t + P], nin[:, b % 2, P * t:P * t + P], sid[:])
                    ins.then_inc(turned, 1)

            @block.scalar
            def _(act):
                for b in range(BATCH):
                    act.wait_ge(ve_ready, b + 1)
                    act.activation(sd[:], mv[:, :, 1], ACT.Sqrt).then_inc(sd_ready, 1)

            @block.vector
            def _(dve):
                for b in range(BATCH):
                    link = chain(dve, step, LINKS * b)
                    y = psM[b % 2][:].rearrange("p (t d) -> p t d", t=KB)
                    dve.wait_ge(turned, b + 1)
                    for t in range(KB):
                        ins = nc.vector.bn_stats(stats[:, t], y[:, t])
                    link(ins)
                    for t in range(KB):
                        ins = nc.vector.bn_aggr(mv[:, t], stats[:, t])
                    link(ins)
                    nc.vector.tensor_scalar(mv[:, :, 1], mv[:, :, 1], EPS_G, None, ALU.add).then_inc(ve_ready, 1)
                    dve.wait_ge(sd_ready, b + 1)
                    link(nc.vector.reciprocal(rs[:], sd[:]))
                    if b >= 2:
                        dve.wait_ge(y_ready, b - 1)
                    for t in range(KB):
                        ins = nc.vector.tensor_scalar(yn[:, b % 2, t], y[:, t], mv[:, t, 0:1], rs[:, t:t + 1],
                                                      ALU.subtract, ALU.mult)
                    ins.then_inc(scaled, 1)
                    dve.wait_ge(scaled, b + 1)

            @block.gpsimd
            def _(pool):
                def each(k):
                    return gb[:, k].unsqueeze(1).to_broadcast([P, KB, DIM])

                def based_on(b):
                    pool.wait_ge(x_in[b], NCHUNK * D16)
                    nc.gpsimd.tensor_tensor(yb[:, b], x1[:, b], each(1), ALU.add).then_inc(based, 1)

                pool.wait_ge(gb_in, 2 * D16)
                based_on(0)
                for b in range(BATCH):
                    if b + 1 < BATCH:
                        based_on(b + 1)
                    pool.wait_ge(scaled, b + 1)
                    nc.gpsimd.tensor_tensor(yn[:, b % 2], yn[:, b % 2], each(0), ALU.mult).then_inc(gained, 1)
                    pool.wait_ge(gained, b + 1)
                    pool.wait_ge(based, b + 1)
                    if b >= 2:
                        pool.wait_ge(y_out, (b - 1) * D16)
                    nc.gpsimd.tensor_tensor(yo[:, b % 2], yn[:, b % 2], yb[:, b], ALU.add).then_inc(y_ready, 1)


_IN = ("L0_attn_x", "L0_attn_W_qk", "L0_attn_W_v", "L0_attn_W_out", "L0_attn_b_out", "L0_attn_conv", "conv_reversed",
       "L0_ffn_ew", "L0_ffn_act_w", "L0_ffn_We", "L0_ffn_be", "L0_ffn_Wq", "L0_ffn_Wk", "L0_ffn_Wv", "L0_ffn_Wo",
       "L0_ffn_ln_g", "L0_ffn_ln_b", "identity", "exchange")


def kernel(**inputs):
    import concourse.bacc as bacc
    from concourse.bass_utils import run_bass_kernel_spmd

    given = {k: np.ascontiguousarray(v) for k, v in inputs.items() if k != "L0_attn_mask"}
    given["conv_reversed"] = np.ascontiguousarray(np.asarray(inputs["L0_attn_conv"])[:, ::-1])
    given["identity"] = np.eye(P, dtype=np.float32)
    given["exchange"] = np.ascontiguousarray(given["identity"][::-1])
    nc = bacc.Bacc("TRN2", target_bir_lowering=False, num_devices=1)
    arrays, args = {}, []
    for name in _IN:
        arrays[f"in_{name}"] = given[name]
        args.append(nc.dram_tensor(f"in_{name}", given[name].shape, F32, kind="ExternalInput").ap())
    out = nc.dram_tensor("out_0", (BATCH, TOK, DIM), F32, kind="ExternalOutput").ap()
    program(nc, *args, out)
    return run_bass_kernel_spmd(nc, [arrays], core_ids=[0]).results[0]["out_0"]
```
